# Optimizing a Trainium2 kernel written in Bass

```python
import numpy as np
import jax
import jax.numpy as jnp

def _softmax(x, axis=-1):
    return jax.nn.softmax(x, axis=axis)

def _gelu(x):
    return jax.nn.gelu(x, approximate=True)

def _silu(x):
    return jax.nn.silu(x)

def _sigmoid(x):
    return jax.nn.sigmoid(x)

def _layernorm(x, axis=-1, eps=1e-05):
    m = jnp.mean(x, axis=axis, keepdims=True)
    v = jnp.var(x, axis=axis, keepdims=True)
    return (x - m) / jnp.sqrt(v + eps)

def _scatter_add(tgt, idx, src, axis=0):
    return tgt.at[idx].add(src)

def _segment_sum(src, seg, n):
    return jax.ops.segment_sum(src, seg, n)
kernel_name = 'mk_adj_resnorm_d2_adj_r2_8bfd2a'

def setup_inputs(seed: int=0):
    np.random.seed(seed)
    _w = jnp.asarray

    def _rec_inputs():
        import jax
        import jax.numpy as jnp
        _gk = jax.random.key(seed)
        x = -0.000929 + 1 * jax.random.normal(jax.random.fold_in(_gk, 1), (2048, 128), jnp.float32)
        _a = jax.random.bernoulli(jax.random.fold_in(_gk, 2), 0.00195312, (2048, 2048))
        _a = jnp.logical_or(_a, jnp.swapaxes(_a, -1, -2))
        _a = jnp.logical_or(_a, jnp.eye(2048, dtype=bool))
        _af = _a.astype(jnp.float32)
        _af = _af * jax.random.uniform(jax.random.fold_in(_gk, 3), (2048, 2048), jnp.float32, 0.05, 1)
        adj = _af
        return (x, adj)
    x, adj = _rec_inputs()

    def _L0_gnn_setup():
        import jax, jax.numpy as jnp
        import numpy as np
        N, H, HEADS = (2048, 128, 3)
        ALPHA = 0.2
        NEG_INF = -9000000000000000.0

        def _sign_adj(key, n, density):
            k1, k2 = jax.random.split(key)
            mask = jax.random.uniform(k1, (n, n)) < density
            sign = jnp.where(jax.random.uniform(k2, (n, n)) < 0.5, -1.0, 1.0)
            adj = jnp.where(mask, sign, 0.0).astype(jnp.float32)
            idx = jnp.arange(n)
            return adj.at[idx, idx].set(1.0)

        def _gru_cell(x, hstate, Wih, Whh, bih, bhh):
            gi = x @ Wih.T + bih
            gh = hstate @ Whh.T + bhh
            ir, iz, inn = jnp.split(gi, 3, axis=1)
            hr, hz, hn = jnp.split(gh, 3, axis=1)
            r = jax.nn.sigmoid(ir + hr)
            z = jax.nn.sigmoid(iz + hz)
            n = jnp.tanh(inn + r * hn)
            return (1.0 - z) * n + z * hstate

        def _gat_head(h, node_adj, edge_adj, W, a):
            hW = h @ W
            hp = (node_adj > 0).astype(hW.dtype) @ hW
            hm = (node_adj < 0).astype(hW.dtype) @ hW
            e_plus = jax.nn.leaky_relu(jnp.concatenate([hp, hm], axis=1) @ a, ALPHA)[:, 0]
            e_minus = jax.nn.leaky_relu(jnp.concatenate([hm, hp], axis=1) @ a, ALPHA)[:, 0]
            att = jnp.where(edge_adj > 0, e_plus[None, :], NEG_INF)
            att = jnp.where(edge_adj < 0, e_minus[None, :], att)
            att = jax.nn.softmax(att, axis=1)
            return att * edge_adj @ hW
        key = jax.random.key(seed)
        ks = jax.random.split(key, 16)
        std = 0.01
        gain = 1.414
        return {'h': jax.random.normal(ks[0], (N, H), jnp.float32), 'node_adj': _sign_adj(ks[1], N, 0.005), 'edge_adj': _sign_adj(ks[2], N, 0.005), 'gat_W': jax.random.normal(ks[3], (HEADS, H, H), jnp.float32) * (gain / np.sqrt(H, dtype=np.float32)), 'gat_a': jax.random.normal(ks[4], (HEADS, 2 * H, 1), jnp.float32) * 0.1, 'edge_Wih': jax.random.normal(ks[5], (3 * H, H), jnp.float32) * std, 'edge_Whh': jax.random.normal(ks[6], (3 * H, H), jnp.float32) * std, 'edge_bih': jnp.zeros((3 * H,), jnp.float32), 'edge_bhh': jnp.zeros((3 * H,), jnp.float32), 'node_Wih': jax.random.normal(ks[7], (3 * H, H), jnp.float32) * std, 'node_Whh': jax.random.normal(ks[8], (3 * H, H), jnp.float32) * std, 'node_bih': jnp.zeros((3 * H,), jnp.float32), 'node_bhh': jnp.zeros((3 * H,), jnp.float32)}
    _L0_gnn_all = _L0_gnn_setup()
    _L0_gnn_in = {k: v for k, v in _L0_gnn_all.items() if k in ('gat_W', 'gat_a', 'edge_Wih', 'edge_Whh', 'edge_bih', 'edge_bhh', 'node_Wih', 'node_Whh', 'node_bih', 'node_bhh')}
    del _L0_gnn_all

    def _L1_gnn_setup():
        import jax, jax.numpy as jnp
        import numpy as np
        N = 4096
        D_IN = 128
        D_OUT = 128
        key = jax.random.key(seed)
        k1, k2, k3, k4 = jax.random.split(key, 4)
        x = jax.random.normal(k1, (N, D_IN), dtype=jnp.float32)
        adj = jax.random.uniform(k2, (N, N), dtype=jnp.float32)
        W = jax.random.normal(k3, (D_OUT, D_IN), dtype=jnp.float32) * (1.0 / np.sqrt(D_IN))
        b = jax.random.normal(k4, (D_OUT,), dtype=jnp.float32) * 0.01
        return {'x': x, 'adj': adj, 'W': W, 'b': b}
    _L1_gnn_all = _L1_gnn_setup()
    _L1_gnn_in = {k: v for k, v in _L1_gnn_all.items() if k in ('W', 'b')}
    del _L1_gnn_all
    return {'x': x, 'adj': adj, 'L0_gnn_gat_W': _L0_gnn_in['gat_W'], 'L0_gnn_gat_a': _L0_gnn_in['gat_a'], 'L0_gnn_edge_Wih': _L0_gnn_in['edge_Wih'], 'L0_gnn_edge_Whh': _L0_gnn_in['edge_Whh'], 'L0_gnn_edge_bih': _L0_gnn_in['edge_bih'], 'L0_gnn_edge_bhh': _L0_gnn_in['edge_bhh'], 'L0_gnn_node_Wih': _L0_gnn_in['node_Wih'], 'L0_gnn_node_Whh': _L0_gnn_in['node_Whh'], 'L0_gnn_node_bih': _L0_gnn_in['node_bih'], 'L0_gnn_node_bhh': _L0_gnn_in['node_bhh'], 'L1_gnn_W': _L1_gnn_in['W'], 'L1_gnn_b': _L1_gnn_in['b']}

def reference(x, adj, L0_gnn_gat_W, L0_gnn_gat_a, L0_gnn_edge_Wih, L0_gnn_edge_Whh, L0_gnn_edge_bih, L0_gnn_edge_bhh, L0_gnn_node_Wih, L0_gnn_node_Whh, L0_gnn_node_bih, L0_gnn_node_bhh, L1_gnn_W, L1_gnn_b):
    import jax
    import jax.numpy as jnp

    def _L0_gnn_ref(h, node_adj, edge_adj, gat_W, gat_a, edge_Wih, edge_Whh, edge_bih, edge_bhh, node_Wih, node_Whh, node_bih, node_bhh):
        import jax, jax.numpy as jnp
        import numpy as np
        N, H, HEADS = (2048, 128, 3)
        ALPHA = 0.2
        NEG_INF = -9000000000000000.0

        def _sign_adj(key, n, density):
            k1, k2 = jax.random.split(key)
            mask = jax.random.uniform(k1, (n, n)) < density
            sign = jnp.where(jax.random.uniform(k2, (n, n)) < 0.5, -1.0, 1.0)
            adj = jnp.where(mask, sign, 0.0).astype(jnp.float32)
            idx = jnp.arange(n)
            return adj.at[idx, idx].set(1.0)

        def _gru_cell(x, hstate, Wih, Whh, bih, bhh):
            gi = x @ Wih.T + bih
            gh = hstate @ Whh.T + bhh
            ir, iz, inn = jnp.split(gi, 3, axis=1)
            hr, hz, hn = jnp.split(gh, 3, axis=1)
            r = jax.nn.sigmoid(ir + hr)
            z = jax.nn.sigmoid(iz + hz)
            n = jnp.tanh(inn + r * hn)
            return (1.0 - z) * n + z * hstate

        def _gat_head(h, node_adj, edge_adj, W, a):
            hW = h @ W
            hp = (node_adj > 0).astype(hW.dtype) @ hW
            hm = (node_adj < 0).astype(hW.dtype) @ hW
            e_plus = jax.nn.leaky_relu(jnp.concatenate([hp, hm], axis=1) @ a, ALPHA)[:, 0]
            e_minus = jax.nn.leaky_relu(jnp.concatenate([hm, hp], axis=1) @ a, ALPHA)[:, 0]
            att = jnp.where(edge_adj > 0, e_plus[None, :], NEG_INF)
            att = jnp.where(edge_adj < 0, e_minus[None, :], att)
            att = jax.nn.softmax(att, axis=1)
            return att * edge_adj @ hW
        dn = jnp.diag(node_adj)
        de = jnp.diag(edge_adj)
        idx = jnp.arange(node_adj.shape[0])
        node_adj_norm = node_adj.at[idx, idx].add(-dn)
        edge_adj_norm = edge_adj.at[idx, idx].add(-de)
        node_support = node_adj_norm @ h
        edge_output = _gru_cell(node_support, h, edge_Wih, edge_Whh, edge_bih, edge_bhh)
        edge_support = _gat_head(h, node_adj_norm, edge_adj_norm, gat_W[0], gat_a[0])
        for i in range(1, HEADS):
            edge_support = edge_support + _gat_head(h, node_adj_norm, edge_adj_norm, gat_W[i], gat_a[i])
        edge_support = edge_support / HEADS
        node_output = _gru_cell(edge_support, h, node_Wih, node_Whh, node_bih, node_bhh)
        return de[:, None] * edge_output + dn[:, None] * node_output

    def _L1_gnn_ref(x, adj, W, b):
        import jax, jax.numpy as jnp
        import numpy as np
        N = 4096
        D_IN = 128
        D_OUT = 128
        h = x @ W.T + b
        A = adj + jnp.eye(adj.shape[0], dtype=adj.dtype)
        rowsum = A.sum(axis=1)
        r_inv_sqrt = jnp.power(rowsum, -0.5)
        r_inv_sqrt = jnp.where(jnp.isinf(r_inv_sqrt), 0.0, r_inv_sqrt)
        A_norm = r_inv_sqrt[:, None] * A * r_inv_sqrt[None, :]
        return A_norm.astype(jnp.float32) @ h.astype(jnp.float32)
    x = _layernorm(x + _L0_gnn_ref(x, adj, adj, L0_gnn_gat_W, L0_gnn_gat_a, L0_gnn_edge_Wih, L0_gnn_edge_Whh, L0_gnn_edge_bih, L0_gnn_edge_bhh, L0_gnn_node_Wih, L0_gnn_node_Whh, L0_gnn_node_bih, L0_gnn_node_bhh), axis=-1)
    x = _layernorm(x + _L1_gnn_ref(x, adj, L1_gnn_W, L1_gnn_b), axis=-1)
    return x

_drawn_inputs = setup_inputs


def setup_inputs(seed=0):
    import zlib

    import numpy as np

    out = dict(_drawn_inputs(seed))
    spreads = {'L0_gnn_edge_bih': (0.0, 0.346),
     'L0_gnn_edge_bhh': (0.0, 0.63),
     'L0_gnn_node_bih': (0.0, 0.371),
     'L0_gnn_node_bhh': (0.0, 0.595)}
    factors = {'L0_gnn_gat_W': 6.563,
     'L0_gnn_gat_a': 7.851,
     'L0_gnn_edge_Whh': 4.178,
     'L0_gnn_node_Wih': 6.59,
     'L0_gnn_node_Whh': 4.13,
     'L1_gnn_b': 5.979}
    for name, (base, spread) in spreads.items():
        noise = np.random.default_rng([zlib.crc32(name.encode()), seed]).standard_normal(out[name].shape)
        drawn = base * np.exp(spread * noise) if base else spread * noise
        out[name] = jnp.asarray(drawn.astype(out[name].dtype))
    for name, factor in factors.items():
        out[name] = (out[name] * factor).astype(out[name].dtype)
    return out
```

```python
from contextlib import ExitStack

import concourse.bass as bass
import numpy as np
from concourse import mybir

P = 128
N = 2048
HEADS = 3
NB = N // P
RING = 4
BANK = 512
NC = N // BANK
TPG = 2
GW = TPG * P
GPB = RING // TPG
BODIES = NB // (TPG * GPB)
STEPS = HEADS * GPB
MICRO = STEPS * TPG
SPLIT = 3
ROWS = 1 + SPLIT * 2 * HEADS
NW = ROWS + 1
ESLOT = 3
TSLOT = 2
BIG = 1e30
ALPHA = 0.2
EPS = 1e-5

ALU = mybir.AluOpType
ACT = mybir.ActivationFunctionType
F32 = mybir.dt.float32
BF16 = mybir.dt.bfloat16
AX_X = mybir.AxisListType.X


def need(eng, sem, value):
    if isinstance(value, int) and value <= 0:
        return
    eng.wait_ge(sem, value)


def build(nc, t):
    with ExitStack() as ctx:
        def sb(name, shape, dt=F32):
            return ctx.enter_context(nc.sbuf_tensor(name, shape, dt))

        def psum(name, shape):
            return ctx.enter_context(nc.psum_tensor(name, shape, F32))

        def sem(name):
            return ctx.enter_context(nc.semaphore(name))

        ring = sb("ring", [P, RING, N])
        x_nat = sb("x_nat", [P, NB, P])
        xT = sb("xT", [P, N])
        nsT = sb("nsT", [P, N])
        supT = sb("supT", [P, N])
        nscore = sb("nscore", [P, 2, HEADS, N])
        mask = sb("mask", [P, RING, N], BF16)
        att = sb("att", [P, ESLOT, N])
        attT = sb("attT", [P, 2, NB, GW])
        ident = sb("ident", [P, P])
        offdiag = sb("offdiag", [P, P])
        gatW = sb("gatW", [P, HEADS, P])
        wih = sb("wih", [P, 2, 3 * P])
        whh = sb("whh", [P, 2, 3 * P])
        bih = sb("bih", [P, 2, 3])
        bhh = sb("bhh", [P, 2, 3])
        gate_b = sb("gate_b", [P, 2, 2])
        l1WT = sb("l1WT", [P, P])
        l1b = sb("l1b", [1, P])
        ones_row = sb("ones_row", [1, P])
        wa = sb("wa", [P, 2, HEADS])
        diag = sb("diag", [P, NB])
        rowsum = sb("rowsum", [P, NB])
        nmin = sb("nmin", [P, ESLOT])
        neg_count = sb("neg_count", [1, 1])
        neg_flag = sb("neg_flag", [1, 1], mybir.dt.int32)
        nmin4 = sb("nmin4", [P, NC])
        pause = sb("pause", [P, 1])
        nmin2 = sb("nmin2", [P, 2])
        den = sb("den", [P, ESLOT])
        rden = sb("rden", [P, ESLOT])
        yh = sb("yh", [P, 2, GW])
        stats = sb("stats", [P, NB, 6])
        mean = sb("mean", [P, NB])
        spread = sb("spread", [P, NB])
        rstd = sb("rstd", [P, NB])
        rinv = sb("rinv", [P, NB])
        tmp16 = sb("tmp16", [P, NB])
        scratch = sb("scratch", [P, N], BF16)
        early = attT[:, :, :, :].rearrange("p a b c -> p (a b c)")
        pos = early[:, 0:N].bitcast(BF16).rearrange("p (s n) -> p s n", s=2)
        neg = early[:, N:2 * N].bitcast(BF16).rearrange("p (s n) -> p s n", s=2)
        uf = early[:, 2 * N:2 * N + NB * 6].rearrange("p (b c) -> p b c", b=NB)
        u1 = early[:, 2 * N + 96:2 * N + 192].rearrange("p (b c) -> p b c", b=NB)
        upos = early[:, 2 * N + 192:2 * N + 192 + NB * NW // 2].bitcast(BF16).rearrange("p (b c) -> p b c", b=NB)
        uneg = early[:, 2 * N + 352:2 * N + 352 + NB * NW // 2].bitcast(BF16).rearrange("p (b c) -> p b c", b=NB)
        x_st = early[:, 2 * N + 512:2 * N + 1024].rearrange("p (s c) -> p s c", s=RING)
        gatWT = early[:, 2 * N + 1024:2 * N + 1408].rearrange("p (h c) -> p h c", h=HEADS)
        gata = early[:, 2 * N + 1408:2 * N + 1414].rearrange("p (h c) -> p h c", h=HEADS)
        sel = att[0:ROWS, 0, 0:6 * P].rearrange("p (c m) -> p c m", c=6)
        score_rows = att[0:ROWS, 1, :]
        g_tr, g_tz, g_hn, g_n = (att[:, 0, BANK * k:BANK * (k + 1)] for k in range(4))
        g_a, g_b, g_d, g_tot = (att[:, 1, BANK * k:BANK * (k + 1)] for k in range(4))
        x1 = early[:, 0:N].rearrange("p (b f) -> p b f", b=NB)
        gmat = early[:, N:2 * N].rearrange("p (b f) -> p b f", b=NB)
        outT = early[:, 2 * N:3 * N]
        g_st = early[:, 3 * N:3 * N + RING * P].rearrange("p (s f) -> p s f", s=RING)
        x1T = early[:, 3 * N + RING * P:3 * N + RING * P + BANK]
        x2 = att[:, 2, :].rearrange("p (b f) -> p b f", b=NB)

        ps = psum("ps", [P, 8, BANK])
        trp = ps[:, 0:2 * TSLOT, :].rearrange("p (s b) (k c) -> p s (b k) c", s=TSLOT, c=P)
        minus = ps[:, 7, :]
        y_ps = ps[:, 4:6, 0:GW]
        s_ps = ps[:, 6, 0:GW]

        names = """consts_in load0 load1 load2 load3 wa_mm wa_ready u_mm u_split upos_ready
            diag_zeroed masks_ready x_staged ns_done mask_mm_done ns_out rows_out bcast_mm nscore_ready
            paused flagged plus_scored minus_step prep mask_ready rowsum_done scored exp_done rden_ready weighted chunk_transposed chunk_evac
            y_ready y_evac s_mm s_evac leaky tiny gru_mm gate_ready rz_done gate_prod n_ready gru_vec gru_out gru_tr
            x1_pre ln_stat ln_var ln_sqrt x1_done rs_in rs_sqrt r_ready x1_tr x1T_out h_mm g_ready g_staged
            conv_done outT_done out_tr mom fin_vec x2_pre ln2_stat ln2_var ln2_sqrt x2_done stored""".split()
        S = {n: sem(n) for n in names}
        loads = [S[f"load{k}"] for k in range(RING)]
        N_CONST = 22

        block = ctx.enter_context(nc.Block())

        @block.sync
        def _(sp):
            small = [(gatWT, t["gat_WT"].rearrange("h k f -> k h f")),
                     (x_nat[:, :, :], t["x"].rearrange("(b p) f -> p b f", p=P)), (xT[:, :], t["xT"]),
                     (sel, t["sel"]), (ident[:, :], t["ident"]), (offdiag[:, :], t["offdiag"]),
                     (gatW[:, :, :], t["gat_W"].rearrange("h k f -> k h f")),
                     (wih[:, 0, :], t["edge_WihT"]), (wih[:, 1, :], t["node_WihT"]),
                     (whh[:, 0, :], t["edge_WhhT"]), (whh[:, 1, :], t["node_WhhT"]),
                     (bih[:, 0, :], t["edge_bih"]), (bih[:, 1, :], t["node_bih"]),
                     (bhh[:, 0, :], t["edge_bhh"]), (bhh[:, 1, :], t["node_bhh"]),
                     (l1WT[:, :], t["l1WT"]), (l1b[:, :], t["l1b"]), (ones_row[:, :], t["ones_row"])]
            small += [(diag[:, :], t["adj_diag"])]
            small += [(gata[:, h, :], t["gat_aT"][:, h, :]) for h in range(HEADS)]
            assert len(small) == N_CONST
            for dst, src in small:
                sp.dma_start(dst, src).then_inc(S["consts_in"], 16)

            def load(slot, src):
                sp.dma_start(ring[:, slot, :], src).then_inc(loads[slot], 16)

            for k in range(RING):
                load(k, t["adjT"][k * P:(k + 1) * P, :])
            with sp.Fori(1, NB // RING) as it:
                for k in range(RING):
                    sp.wait_ge(S["mask_mm_done"], RING * it - RING + k + 1)
                    load(k, t["adjT"][bass.ds(it * (RING * P) + k * P, P), :])
            for k in range(RING):
                sp.wait_ge(S["mask_mm_done"], NB - RING + k + 1)
                load(k, t["adj"][k * P:(k + 1) * P, :])

            def last_weighting(body, k):
                g, tile = divmod(k, TPG)
                return body * MICRO + (g * HEADS + HEADS - 1) * TPG + tile + 1

            with sp.Fori(1, BODIES) as it:
                for k in range(RING):
                    sp.wait_ge(S["weighted"], last_weighting(it - 1, k))
                    load(k, t["adj"][bass.ds(it * (RING * P) + k * P, P), :])
            for k in range(RING):
                sp.wait_ge(S["weighted"], last_weighting(BODIES - 1, k))
                load(k, t["adjT"][k * P:(k + 1) * P, :])
            with sp.Fori(1, NB // RING) as it:
                for k in range(RING):
                    sp.wait_ge(S["conv_done"], RING * it - RING + k + 1)
                    load(k, t["adjT"][bass.ds(it * (RING * P) + k * P, P), :])
            sp.wait_ge(S["x2_done"], NB)
            sp.dma_start(t["out"].rearrange("(b p) f -> p b f", p=P), x2).then_inc(S["stored"], 16)
            sp.wait_ge(S["stored"], 16)

        @block.gpsimd
        def _(pool):
            pool.wait_ge(S["consts_in"], 16 * N_CONST)

            def stage_x(it):
                for k in range(RING):
                    need(pool, S["ns_done"], RING * it - RING + k + 1)
                    nc.gpsimd.tensor_copy(x_st[:, k, :], x_nat[:, bass.ds(RING * it + k, 1), :].rearrange(
                        "p o f -> p (o f)")).then_inc(S["x_staged"], 1)
            stage_x(0)
            with pool.Fori(1, NB // RING) as it:
                stage_x(it)

            def stage_g(it):
                for k in range(RING):
                    pool.wait_ge(S["g_ready"], RING * it + k + 1)
                    need(pool, S["conv_done"], RING * it - RING + k + 1)
                    nc.gpsimd.tensor_copy(g_st[:, k, :], gmat[:, bass.ds(RING * it + k, 1), :].rearrange(
                        "p o f -> p (o f)")).then_inc(S["g_staged"], 1)
            stage_g(0)
            with pool.Fori(1, NB // RING) as it:
                stage_g(it)

        @block.scalar
        def _(act):
            act.wait_ge(S["wa_mm"], 1)
            nc.scalar.activation(wa[:, :, :], ps[:, 4, 0:6].rearrange("p (h s) -> p s h", s=2),
                                 ACT.Copy).then_inc(S["wa_ready"], 1)
            act.wait_ge(S["mask_mm_done"], NB)
            nc.scalar.activation(score_rows, ps[0:ROWS, 4:8, :].rearrange("p b c -> p (b c)"),
                                 ACT.Copy).then_inc(S["rows_out"], 1)
            nc.scalar.activation(nsT[:, :], ps[:, 0:4, :].rearrange("p b c -> p (b c)"),
                                 ACT.Copy).then_inc(S["ns_out"], 1)
            for c in range(2 * HEADS):
                s, h = divmod(c, HEADS)
                bank = 4 * ((c + 1) % 2)
                act.wait_ge(S["bcast_mm"], c + 1)
                nc.scalar.activation(nscore[:, s, h, :], ps[:, bank:bank + 4, :].rearrange("p b c -> p (b c)"),
                                     ACT.Copy, scale=-1.0).then_inc(S["nscore_ready"], 1)

            def transposed_out(step, sl, tile):
                q, ql = TPG * step + tile, TPG * sl + tile
                need(act, S["y_ready"], step - 1)
                for c in range(2):
                    slot = (2 * ql + c) % TSLOT
                    act.wait_ge(S["chunk_transposed"], 2 * q + c + 1)
                    nc.scalar.activation(attT[:, sl % 2, 8 * c:8 * c + 8, tile * P:(tile + 1) * P],
                                         trp[:, slot, :, :], ACT.Copy).then_inc(S["chunk_evac"], 1)

            def y_out(step, sl):
                act.wait_ge(S["y_ready"], step + 1)
                need(act, S["s_mm"], step - 1)
                nc.scalar.activation(yh[:, sl % 2, :], y_ps[:, sl % 2, :], ACT.Copy).then_inc(S["y_evac"], 1)

            def s_out(group, gl):
                act.wait_ge(S["s_mm"], HEADS * group + HEADS)
                nc.scalar.activation(supT[:, bass.ds(group * GW, GW)], s_ps, ACT.Copy,
                                     scale=1.0 / HEADS).then_inc(S["s_evac"], 1)

            def lagged(it, sl, tile, first):
                if not first or sl >= 1:
                    transposed_out(STEPS * it + sl - 1, (sl - 1) % STEPS, tile)
                if tile == 0 and (not first or sl >= 2):
                    y_out(STEPS * it + sl - 2, (sl - 2) % STEPS)
                if tile == 0 and sl % HEADS == 2 and (not first or sl >= 3 + 2):
                    s_out(GPB * it + sl // HEADS - 1, (sl // HEADS - 1) % GPB)

            def attention(it, first):
                for p in range(MICRO):
                    sl, tile = divmod(p, TPG)
                    gl, h = divmod(sl, HEADS)
                    q = MICRO * it + p
                    if h == 0:
                        rs = gl * TPG + tile
                        i = RING * it + rs
                        act.wait_ge(S["prep"], i + 1)
                        need(act, S["rowsum_done"], i)
                        nc.scalar.activation(scratch[:, :], ring[:, rs, :], ACT.Copy,
                                             accum_out=rowsum[:, bass.ds(i, 1)]).then_inc(S["rowsum_done"], 1)
                    e = p % ESLOT
                    act.wait_ge(S["scored"], q + 1)
                    nc.scalar.activation(att[:, e, :], att[:, e, :], ACT.Exp, bias=nmin[:, e:e + 1], scale=-1.0,
                                         accum_out=den[:, e:e + 1]).then_inc(S["exp_done"], 1)
                    lagged(it, sl, tile, first)
            attention(0, True)
            with act.Fori(1, BODIES) as it:
                attention(it, False)
            for sl in range(3):
                for tile in range(TPG):
                    if sl == 0:
                        transposed_out(STEPS * BODIES - 1, STEPS - 1, tile)
                if sl <= 1:
                    y_out(STEPS * BODIES + sl - 2, (sl - 2) % STEPS)
                if sl == 2:
                    s_out(GPB * BODIES - 1, GPB - 1)

            def gru(c):
                for k in range(2):
                    u = 2 * c + k
                    act.wait_ge(S["gru_mm"], u + 1)
                    need(act, S["gru_vec"], 6 * u)
                    nc.scalar.activation(g_tr, ps[:, 0, :], ACT.Tanh, bias=gate_b[:, k, 0:1],
                                         scale=0.5).then_inc(S["rz_done"], 1)
                    nc.scalar.activation(g_hn, ps[:, 3, :], ACT.Identity, bias=bhh[:, k, 2:3],
                                         scale=1.0).then_inc(S["rz_done"], 1)
                    nc.scalar.activation(g_tz, ps[:, 1, :], ACT.Tanh, bias=gate_b[:, k, 1:2],
                                         scale=0.5).then_inc(S["rz_done"], 1)
                    act.wait_ge(S["gate_prod"], 2 * u + 2)
                    nc.scalar.activation(g_n, g_b, ACT.Tanh, bias=bih[:, k, 2:3], scale=1.0).then_inc(S["n_ready"], 1)
            act.wait_ge(S["gate_ready"], 1)
            gru(0)
            with act.Fori(1, NC) as c:
                gru(c)
            act.wait_ge(S["ln_var"], 6)
            nc.scalar.activation(rstd[:, :], rstd[:, :], ACT.Sqrt).then_inc(S["ln_sqrt"], 1)
            act.wait_ge(S["rs_in"], 1)
            nc.scalar.activation(rinv[:, :], rowsum[:, :], ACT.Sqrt).then_inc(S["rs_sqrt"], 1)
            for c in range(NC):
                act.wait_ge(S["x1_tr"], c + 1)
                need(act, S["h_mm"], c)
                nc.scalar.activation(x1T, ps[:, 4, :], ACT.Copy).then_inc(S["x1T_out"], 1)
            act.wait_ge(S["conv_done"], NB)
            nc.scalar.activation(outT, ps[:, 0:4, :].rearrange("p b c -> p (b c)"), ACT.Copy).then_inc(S["outT_done"], 1)
            act.wait_ge(S["ln2_var"], 6)
            nc.scalar.activation(rstd[:, :], rstd[:, :], ACT.Sqrt).then_inc(S["ln2_sqrt"], 1)

        @block.vector
        def _(dve):
            V = nc.vector
            dve.wait_ge(S["consts_in"], 16 * N_CONST)
            V.tensor_tensor(gate_b[:, :, :], bih[:, :, 0:2], bhh[:, :, 0:2], ALU.add).then_inc(S["tiny"], 1)
            dve.wait_ge(S["tiny"], 1)
            V.tensor_scalar(gate_b[:, :, :], gate_b[:, :, :], 0.5, None, ALU.mult).then_inc(S["gate_ready"], 1)
            dve.wait_ge(S["u_mm"], 1)
            V.tensor_copy(uf, ps[:, 5, 0:NB * 6].rearrange("p (b c) -> p b c", b=NB)).then_inc(S["u_split"], 1)
            V.memset(upos[:, :, 0:1], 0.0).then_inc(S["upos_ready"], 1)
            V.memset(uneg[:, :, 0:1], 1.0).then_inc(S["upos_ready"], 1)
            count = 1
            for k in range(SPLIT):
                dve.wait_ge(S["u_split"], count)
                part = upos[:, :, 1 + 6 * k:7 + 6 * k]
                V.tensor_copy(part, uf).then_inc(S["u_split"], 1)
                count += 1
                dve.wait_ge(S["u_split"], count)
                if k < SPLIT - 1:
                    V.tensor_tensor(uf, uf, part, ALU.subtract).then_inc(S["u_split"], 1)
                    count += 1
                for s in range(2):
                    V.tensor_copy(uneg[:, :, 1 + 6 * k + 3 * s:4 + 6 * k + 3 * s],
                                  upos[:, :, 4 + 6 * k - 3 * s:7 + 6 * k - 3 * s]).then_inc(S["upos_ready"], 1)

            def pass1(it):
                for k in range(RING):
                    jb = RING * it + k
                    dve.wait_ge(loads[k], 16 * (it + 1))
                    d = ring[:, k, bass.ds(jb * P, P)]
                    V.tensor_tensor(d, d, offdiag[:, :], ALU.mult).then_inc(S["diag_zeroed"], 1)
                    dve.wait_ge(S["diag_zeroed"], jb + 1)
                    need(dve, S["mask_mm_done"], jb - 1)
                    V.tensor_scalar(pos[:, k % 2, :], ring[:, k, :], 0.0, None, ALU.is_gt).then_inc(S["masks_ready"], 1)
                    V.tensor_scalar(neg[:, k % 2, :], ring[:, k, :], 0.0, None, ALU.is_lt).then_inc(S["masks_ready"], 1)
            pass1(0)
            with dve.Fori(1, NB // RING) as it:
                pass1(it)
            for c in range(2 * HEADS):
                s, h = divmod(c, HEADS)
                dve.wait_ge(S["nscore_ready"], c + 1)
                n = nscore[:, s, h, :]
                V.scalar_tensor_tensor(out=n, in0=n, scalar=ALPHA, in1=n, op0=ALU.mult,
                                       op1=ALU.min).then_inc(S["leaky"], 1)

            def prepare(it, rs):
                i = RING * it + rs
                dve.wait_ge(loads[rs], 16 * (NB // RING + 1 + it))
                d = ring[:, rs, bass.ds(i * P, P)]
                V.tensor_tensor(d, d, offdiag[:, :], ALU.mult).then_inc(S["prep"], 1)
                dve.wait_ge(S["prep"], i + 1)
                V.tensor_scalar(mask[:, rs, :], ring[:, rs, :], 0.0, BIG, ALU.is_le, ALU.mult).then_inc(S["mask_ready"], 1)

            def score_negative(it, p):
                sl, tile = divmod(p, TPG)
                gl, h = divmod(sl, HEADS)
                rs, e, q = gl * TPG + tile, p % ESLOT, MICRO * it + p
                done = 4 * NC * q + q
                dve.wait_ge(S["plus_scored"], q + 1)
                for c in range(NC):
                    cols = slice(c * BANK, (c + 1) * BANK)
                    need(dve, S["minus_step"], done + 4 * c)
                    V.tensor_scalar(minus, ring[:, rs, cols], 0.0, BIG, ALU.is_ge, ALU.mult).then_inc(S["minus_step"], 1)
                    dve.wait_ge(S["minus_step"], done + 4 * c + 1)
                    V.tensor_tensor(minus, minus, nscore[:, 1, h, cols], ALU.add).then_inc(S["minus_step"], 1)
                    dve.wait_ge(S["minus_step"], done + 4 * c + 2)
                    V.tensor_reduce(nmin4[:, c:c + 1], minus, AX_X, ALU.min).then_inc(S["minus_step"], 1)
                    dve.wait_ge(S["minus_step"], done + 4 * c + 3)
                    V.tensor_tensor(att[:, e, cols], att[:, e, cols], minus, ALU.min).then_inc(S["minus_step"], 1)
                dve.wait_ge(S["minus_step"], done + 4 * NC)
                V.tensor_reduce(nmin2[:, 0:1], nmin4[:, :], AX_X, ALU.min).then_inc(S["minus_step"], 1)
                dve.wait_ge(S["minus_step"], done + 4 * NC + 1)
                V.tensor_tensor(nmin[:, e:e + 1], nmin[:, e:e + 1], nmin2[:, 0:1], ALU.min).then_inc(S["scored"], 1)

            def score(it, p, signed):
                sl, tile = divmod(p, TPG)
                gl, h = divmod(sl, HEADS)
                rs, e, q = gl * TPG + tile, p % ESLOT, MICRO * it + p
                if h == 0:
                    prepare(it, rs)
                dve.wait_ge(S["mask_ready"], RING * it + rs + 1)
                need(dve, S["chunk_transposed"], 2 * (q - ESLOT) + 2)
                need(dve, S["paused"], q)
                V.memset(pause[:, :], 0.0).then_inc(S["paused"], 1)
                V.tensor_tensor_reduce(att[:, e, :], mask[:, rs, :], nscore[:, 0, h, :], 1.0, 3e38, ALU.add,
                                       ALU.min, nmin[:, e:e + 1]).then_inc(S["plus_scored" if signed else "scored"], 1)
                if signed:
                    score_negative(it, p)

            def weight(q, p):
                sl, tile = divmod(p, TPG)
                rs, e = (sl // HEADS) * TPG + tile, p % ESLOT
                dve.wait_ge(S["exp_done"], q + 1)
                V.reciprocal(rden[:, e:e + 1], den[:, e:e + 1]).then_inc(S["rden_ready"], 1)
                dve.wait_ge(S["rden_ready"], q + 1)
                V.scalar_tensor_tensor(out=att[:, e, :], in0=att[:, e, :], scalar=rden[:, e:e + 1],
                                       in1=ring[:, rs, :], op0=ALU.mult, op1=ALU.mult).then_inc(S["weighted"], 1)

            def attention(it, first, signed):
                for p in range(MICRO):
                    score(it, p, signed)
                    if not (first and p == 0):
                        weight(MICRO * it + p - 1, (p - 1) % MICRO)
            dve.wait_ge(S["leaky"], 2 * HEADS)
            dve.wait_ge(S["rows_out"], 1)
            V.tensor_reduce(neg_count[:, :], score_rows[0:1, :], AX_X, ALU.max).then_inc(S["flagged"], 1)
            dve.wait_ge(S["flagged"], 1)
            V.tensor_copy(neg_flag[:, :], neg_count[:, :]).then_inc(S["flagged"], 1)
            dve.wait_ge(S["flagged"], 2)
            any_negative = dve.value_load(neg_flag[0:1, 0:1], min_val=0, max_val=N)
            with dve.If(any_negative > 0):
                attention(0, True, True)
                with dve.Fori(1, BODIES) as it:
                    attention(it, False, True)
            with dve.Else():
                attention(0, True, False)
                with dve.Fori(1, BODIES) as it:
                    attention(it, False, False)
            weight(MICRO * BODIES - 1, MICRO - 1)

            def moments(done):
                V.tensor_tensor(mean[:, :], stats[:, :, 1], stats[:, :, 4], ALU.add).then_inc(S[done], 1)
                V.tensor_tensor(spread[:, :], stats[:, :, 1], stats[:, :, 4], ALU.subtract).then_inc(S[done], 1)
                V.tensor_tensor(rstd[:, :], stats[:, :, 2], stats[:, :, 5], ALU.add).then_inc(S[done], 1)
                dve.wait_ge(S[done], 3)
                V.scalar_tensor_tensor(out=spread[:, :], in0=spread[:, :], scalar=0.25, in1=spread[:, :],
                                       op0=ALU.mult, op1=ALU.mult).then_inc(S[done], 1)
                V.tensor_scalar(mean[:, :], mean[:, :], 0.5, None, ALU.mult).then_inc(S[done], 1)
                V.tensor_scalar(rstd[:, :], rstd[:, :], 1.0 / P, EPS, ALU.mult, ALU.add).then_inc(S["mom"], 1)
                dve.wait_ge(S[done], 4)
                dve.wait_ge(S["mom"], 1 if done == "ln_var" else 2)
                V.tensor_tensor(rstd[:, :], rstd[:, :], spread[:, :], ALU.add).then_inc(S[done], 1)

            def gru(c):
                for k in range(2):
                    u = 2 * c + k
                    base = 6 * u
                    cols = bass.ds(c * BANK, BANK)
                    dve.wait_ge(S["rz_done"], 3 * u + 3)
                    V.scalar_tensor_tensor(out=g_a, in0=g_tr, scalar=1.0, in1=g_hn, op0=ALU.add,
                                           op1=ALU.mult).then_inc(S["gate_prod"], 1)
                    dve.wait_ge(S["gate_prod"], 2 * u + 1)
                    V.scalar_tensor_tensor(out=g_b, in0=g_a, scalar=0.5, in1=ps[:, 2, :], op0=ALU.mult,
                                           op1=ALU.add).then_inc(S["gate_prod"], 1)
                    dve.wait_ge(S["n_ready"], u + 1)
                    V.tensor_tensor(g_d, xT[:, cols], g_n, ALU.subtract).then_inc(S["gru_vec"], 1)
                    dve.wait_ge(S["gru_vec"], base + 1)
                    V.scalar_tensor_tensor(out=g_d, in0=g_tz, scalar=1.0, in1=g_d, op0=ALU.add,
                                           op1=ALU.mult).then_inc(S["gru_vec"], 1)
                    dve.wait_ge(S["gru_vec"], base + 2)
                    if k == 0:
                        need(dve, S["gru_tr"], c)
                        V.scalar_tensor_tensor(out=g_tot, in0=g_d, scalar=0.5, in1=g_n, op0=ALU.mult,
                                               op1=ALU.add).then_inc(S["gru_vec"], 1)
                        dve.wait_ge(S["gru_vec"], base + 3)
                        for _ in range(3):
                            dve.sem_inc(S["gru_vec"], 1)
                    else:
                        V.scalar_tensor_tensor(out=g_d, in0=g_d, scalar=0.5, in1=g_n, op0=ALU.mult,
                                               op1=ALU.add).then_inc(S["gru_vec"], 1)
                        dve.wait_ge(S["gru_vec"], base + 3)
                        V.tensor_tensor(g_tot, g_tot, g_d, ALU.add).then_inc(S["gru_vec"], 1)
                        dve.wait_ge(S["gru_vec"], base + 4)
                        for _ in range(2):
                            dve.sem_inc(S["gru_vec"], 1)
                dve.wait_ge(S["gru_tr"], c + 1)
                for b in range(4):
                    i = 4 * c + b
                    V.scalar_tensor_tensor(out=x1[:, bass.ds(i, 1), :].rearrange("p o f -> p (o f)"),
                                           in0=ps[:, 4, b * P:(b + 1) * P], scalar=diag[:, bass.ds(i, 1)],
                                           in1=x_nat[:, bass.ds(i, 1), :].rearrange("p o f -> p (o f)"),
                                           op0=ALU.mult, op1=ALU.add).then_inc(S["x1_pre"], 1)
                for b in range(4):
                    i = 4 * c + b
                    dve.wait_ge(S["x1_pre"], i + 1)
                    V.bn_stats(stats[:, bass.ds(i, 1), :].rearrange("p o f -> p (o f)"),
                               x1[:, bass.ds(i, 1), :].rearrange("p o f -> p (o f)")).then_inc(S["ln_stat"], 1)
            gru(0)
            with dve.Fori(1, NC) as c:
                gru(c)
            dve.wait_ge(S["ln_stat"], NB)
            moments("ln_var")
            dve.wait_ge(S["rowsum_done"], NB)
            V.scalar_tensor_tensor(out=rowsum[:, :], in0=diag[:, :], scalar=1.0, in1=rowsum[:, :], op0=ALU.add,
                                   op1=ALU.add).then_inc(S["rs_in"], 1)
            dve.wait_ge(S["ln_sqrt"], 1)
            V.reciprocal(rstd[:, :], rstd[:, :]).then_inc(S["x1_done"], 1)
            dve.wait_ge(S["x1_done"], 1)
            for i in range(NB):
                V.tensor_scalar(x1[:, i, :], x1[:, i, :], mean[:, i:i + 1], rstd[:, i:i + 1], ALU.subtract,
                                ALU.mult).then_inc(S["x1_done"], 1)
            dve.wait_ge(S["rs_sqrt"], 1)
            V.tensor_scalar(tmp16[:, :], rinv[:, :], 0.0, None, ALU.is_equal).then_inc(S["r_ready"], 1)
            dve.wait_ge(S["r_ready"], 1)
            V.tensor_tensor(rinv[:, :], rinv[:, :], tmp16[:, :], ALU.add).then_inc(S["r_ready"], 1)
            dve.wait_ge(S["r_ready"], 2)
            V.reciprocal(rinv[:, :], rinv[:, :]).then_inc(S["r_ready"], 1)
            dve.wait_ge(S["r_ready"], 3)
            V.tensor_scalar(tmp16[:, :], tmp16[:, :], -1.0, 1.0, ALU.mult, ALU.add).then_inc(S["r_ready"], 1)
            dve.wait_ge(S["r_ready"], 4)
            V.tensor_tensor(rinv[:, :], rinv[:, :], tmp16[:, :], ALU.mult).then_inc(S["r_ready"], 1)
            dve.wait_ge(S["r_ready"], 5)
            with dve.Fori(0, NC) as c:
                dve.wait_ge(S["h_mm"], c + 1)
                for b in range(4):
                    i = 4 * c + b
                    V.tensor_scalar(gmat[:, bass.ds(i, 1), :].rearrange("p o f -> p (o f)"),
                                    ps[:, 5, b * P:(b + 1) * P], rinv[:, bass.ds(i, 1)], None,
                                    ALU.mult).then_inc(S["g_ready"], 1)
            with dve.Fori(0, NC) as c:
                dve.wait_ge(S["out_tr"], c + 1)
                cnt = 4 * c
                for b in range(4):
                    i = 4 * c + b
                    o = x2[:, bass.ds(i, 1), :].rearrange("p o f -> p (o f)")
                    V.tensor_tensor(o, ps[:, 4, b * P:(b + 1) * P],
                                    gmat[:, bass.ds(i, 1), :].rearrange("p o f -> p (o f)"), ALU.add).then_inc(S["fin_vec"], 1)
                for b in range(4):
                    i = 4 * c + b
                    o = x2[:, bass.ds(i, 1), :].rearrange("p o f -> p (o f)")
                    dve.wait_ge(S["fin_vec"], i + 1)
                    V.scalar_tensor_tensor(out=o, in0=o, scalar=rinv[:, bass.ds(i, 1)],
                                           in1=x1[:, bass.ds(i, 1), :].rearrange("p o f -> p (o f)"),
                                           op0=ALU.mult, op1=ALU.add).then_inc(S["x2_pre"], 1)
                for b in range(4):
                    i = 4 * c + b
                    o = x2[:, bass.ds(i, 1), :].rearrange("p o f -> p (o f)")
                    dve.wait_ge(S["x2_pre"], i + 1)
                    V.bn_stats(stats[:, bass.ds(i, 1), :].rearrange("p o f -> p (o f)"), o).then_inc(S["ln2_stat"], 1)
            dve.wait_ge(S["ln2_stat"], NB)
            moments("ln2_var")
            dve.wait_ge(S["ln2_sqrt"], 1)
            V.reciprocal(rstd[:, :], rstd[:, :]).then_inc(S["ln2_stat"], 1)
            dve.wait_ge(S["ln2_stat"], NB + 1)
            for i in range(NB):
                V.tensor_scalar(x2[:, i, :], x2[:, i, :], mean[:, i:i + 1], rstd[:, i:i + 1], ALU.subtract,
                                ALU.mult).then_inc(S["x2_done"], 1)

        @block.tensor
        def _(pe):
            mm = nc.tensor.matmul
            pe.wait_ge(S["consts_in"], 16 * N_CONST)
            for h in range(HEADS):
                last = mm(ps[:, 4, 2 * h:2 * h + 2], gatWT[:, h, :], gata[:, h, :], start=True, stop=True)
            last.then_inc(S["wa_mm"], 1)
            pe.wait_ge(S["wa_ready"], 1)
            wa_cols = wa[:, :, :].rearrange("p s h -> p (s h)")
            for b in range(NB):
                last = mm(ps[:, 5, 6 * b:6 * b + 6], xT[:, b * P:(b + 1) * P], wa_cols, start=True, stop=True)
            last.then_inc(S["u_mm"], 1)

            def pass1(it, first):
                for k in range(RING):
                    jb = RING * it + k
                    start = first and k == 0
                    pe.wait_ge(S["x_staged"], jb + 1)
                    pe.wait_ge(S["diag_zeroed"], jb + 1)
                    for c in range(NC):
                        last = mm(ps[:, c, :], x_st[:, k, :], ring[:, k, c * BANK:(c + 1) * BANK], start=start,
                                  stop=True, skip_group_check=True)
                    last.then_inc(S["ns_done"], 1)
                    if start:
                        pe.wait_ge(S["upos_ready"], 2 * SPLIT + 2)
                    for sgn, (u, m) in enumerate(((upos, pos), (uneg, neg))):
                        pe.wait_ge(S["masks_ready"], 2 * jb + 1 + sgn)
                        for c in range(NC):
                            last = mm(ps[0:ROWS, 4 + c, :],
                                      u[:, bass.ds(jb, 1), 0:ROWS].rearrange("p o c -> p (o c)"),
                                      m[:, k % 2, c * BANK:(c + 1) * BANK], start=start and sgn == 0, stop=True,
                                      skip_group_check=True)
                    last.then_inc(S["mask_mm_done"], 1)
            pass1(0, True)
            with pe.Fori(1, NB // RING) as it:
                pass1(it, False)
            pe.wait_ge(S["rows_out"], 1)
            for c in range(2 * HEADS):
                bank = 4 * ((c + 1) % 2)
                if c == 1:
                    pe.wait_ge(S["ns_out"], 1)
                need(pe, S["nscore_ready"], c - 1)
                for k in range(NC):
                    last = mm(ps[:, bank + k, :], sel[:, c, :], score_rows[:, k * BANK:(k + 1) * BANK],
                              start=True, stop=True)
                last.then_inc(S["bcast_mm"], 1)

            def transpose_tile(q, ql):
                pe.wait_ge(S["weighted"], q + 1)
                for c in range(2):
                    C = 2 * q + c
                    need(pe, S["chunk_evac"], C - TSLOT + 1)
                    for b in range(8):
                        j = 8 * c + b
                        last = nc.tensor.transpose(trp[:, (2 * ql + c) % TSLOT, b, :],
                                                   att[:, ql % ESLOT, j * P:(j + 1) * P], ident[:, :])
                    last.then_inc(S["chunk_transposed"], 1)

            def product(step, sl, half):
                if half == 0:
                    need(pe, S["y_evac"], step - 1)
                pe.wait_ge(S["chunk_evac"], 4 * step + 3 + half)
                for b in range(8):
                    j = 8 * half + b
                    last = mm(y_ps[:, sl % 2, :], x_nat[:, j, :], attT[:, sl % 2, j, :], start=j == 0,
                              stop=j == NB - 1, skip_group_check=True)
                if half:
                    last.then_inc(S["y_ready"], 1)

            def project(step, sl, group):
                gl, h = divmod(sl, HEADS)
                pe.wait_ge(S["y_evac"], step + 1)
                if h == 0:
                    need(pe, S["s_evac"], group)
                mm(s_ps, gatW[:, h, :], yh[:, sl % 2, :], start=h == 0, stop=h == HEADS - 1,
                   skip_group_check=True).then_inc(S["s_mm"], 1)

            def attention(it, first):
                for p in range(MICRO):
                    sl, tile = divmod(p, TPG)
                    transpose_tile(MICRO * it + p, p)
                    if not first or sl >= 1:
                        product(STEPS * it + sl - 1, (sl - 1) % STEPS, tile)
                    if tile and (not first or sl >= 2):
                        m = (sl - 2) % STEPS
                        project(STEPS * it + sl - 2, m, GPB * it + (sl - 2) // HEADS)
            pe.wait_ge(S["nscore_ready"], 2 * HEADS)
            attention(0, True)
            with pe.Fori(1, BODIES) as it:
                attention(it, False)
            end = STEPS * BODIES
            product(end - 1, STEPS - 1, 0)
            product(end - 1, STEPS - 1, 1)
            project(end - 2, STEPS - 2, GPB * BODIES - 1)
            project(end - 1, STEPS - 1, GPB * BODIES - 1)
            pe.wait_ge(S["s_evac"], GPB * BODIES)

            def gru(c):
                cols = bass.ds(c * BANK, BANK)
                for k in range(2):
                    inp = (nsT, supT)[k]
                    u = 2 * c + k
                    need(pe, S["gate_prod"], 2 * u)
                    need(pe, S["rz_done"], 3 * u)
                    for g in range(2):
                        mm(ps[:, g, :], wih[:, k, g * P:(g + 1) * P], inp[:, cols], start=True, stop=False)
                        mm(ps[:, g, :], whh[:, k, g * P:(g + 1) * P], xT[:, cols], start=False, stop=True)
                    mm(ps[:, 2, :], wih[:, k, 2 * P:3 * P], inp[:, cols], start=True, stop=True)
                    mm(ps[:, 3, :], whh[:, k, 2 * P:3 * P], xT[:, cols], start=True,
                       stop=True).then_inc(S["gru_mm"], 1)
                pe.wait_ge(S["gru_vec"], 12 * c + 12)
                need(pe, S["x1_pre"], 4 * c)
                for b in range(4):
                    last = nc.tensor.transpose(ps[:, 4, b * P:(b + 1) * P], g_tot[:, b * P:(b + 1) * P], ident[:, :])
                last.then_inc(S["gru_tr"], 1)
            gru(0)
            with pe.Fori(1, NC) as c:
                gru(c)

            pe.wait_ge(S["x1_done"], NB + 1)
            for c in range(NC):
                need(pe, S["x1T_out"], c)
                for b in range(4):
                    last = nc.tensor.transpose(
                        ps[:, 4, b * P:(b + 1) * P],
                        x1[:, 4 * c + b, :], ident[:, :])
                last.then_inc(S["x1_tr"], 1)
                pe.wait_ge(S["x1T_out"], c + 1)
                need(pe, S["g_ready"], 4 * c)
                for b in range(4):
                    mm(ps[:, 5, b * P:(b + 1) * P], x1T[:, b * P:(b + 1) * P], l1WT[:, :], start=True, stop=False,
                       skip_group_check=True)
                    last = mm(ps[:, 5, b * P:(b + 1) * P], ones_row[:, :], l1b[:, :], start=False, stop=True,
                              skip_group_check=True)
                last.then_inc(S["h_mm"], 1)

            def conv(it, first):
                for k in range(RING):
                    jb = RING * it + k
                    pe.wait_ge(S["g_staged"], jb + 1)
                    pe.wait_ge(loads[k], 16 * (2 * (NB // RING) + it + 1))
                    for c in range(NC):
                        last = mm(ps[:, c, :], g_st[:, k, :], ring[:, k, c * BANK:(c + 1) * BANK],
                                  start=first and k == 0, stop=True, skip_group_check=True)
                    last.then_inc(S["conv_done"], 1)
            conv(0, True)
            with pe.Fori(1, NB // RING) as it:
                conv(it, False)
            pe.wait_ge(S["outT_done"], 1)
            for c in range(NC):
                need(pe, S["fin_vec"], 4 * c)
                for b in range(4):
                    last = nc.tensor.transpose(ps[:, 4, b * P:(b + 1) * P],
                                               outT[:, c * BANK + b * P:c * BANK + (b + 1) * P], ident[:, :])
                last.then_inc(S["out_tr"], 1)


def kernel(x, adj, L0_gnn_gat_W, L0_gnn_gat_a, L0_gnn_edge_Wih, L0_gnn_edge_Whh, L0_gnn_edge_bih, L0_gnn_edge_bhh,
           L0_gnn_node_Wih, L0_gnn_node_Whh, L0_gnn_node_bih, L0_gnn_node_bhh, L1_gnn_W, L1_gnn_b):
    import concourse.bacc as bacc
    from concourse.bass_utils import run_bass_kernel_spmd

    C = np.ascontiguousarray
    adj = np.asarray(adj)
    x = np.asarray(x)
    eye = np.eye(P, dtype=np.float32)
    sel = np.zeros((ROWS, 2 * HEADS, P), np.float32)
    for r in range(ROWS):
        if r:
            sel[r, (r - 1) % (2 * HEADS), :] = 1.0
    arrays = {
        "x": C(x), "xT": C(x.T), "adj": C(adj), "adjT": C(adj.T),
        "adj_diag": C(adj.diagonal().reshape(NB, P).T),
        "gat_W": C(L0_gnn_gat_W), "gat_WT": C(np.asarray(L0_gnn_gat_W).transpose(0, 2, 1)),
        "gat_aT": C(np.asarray(L0_gnn_gat_a).reshape(HEADS, 2, P).transpose(2, 0, 1)),
        "edge_WihT": C(np.asarray(L0_gnn_edge_Wih).T), "edge_WhhT": C(np.asarray(L0_gnn_edge_Whh).T),
        "node_WihT": C(np.asarray(L0_gnn_node_Wih).T), "node_WhhT": C(np.asarray(L0_gnn_node_Whh).T),
        "edge_bih": C(np.asarray(L0_gnn_edge_bih).reshape(3, P).T),
        "edge_bhh": C(np.asarray(L0_gnn_edge_bhh).reshape(3, P).T),
        "node_bih": C(np.asarray(L0_gnn_node_bih).reshape(3, P).T),
        "node_bhh": C(np.asarray(L0_gnn_node_bhh).reshape(3, P).T),
        "l1WT": C(np.asarray(L1_gnn_W).T), "l1b": C(np.asarray(L1_gnn_b).reshape(1, P)),
        "ident": eye, "offdiag": np.ones((P, P), np.float32) - eye, "sel": sel,
        "ones_row": np.ones((1, P), np.float32),
    }
    nc = bacc.Bacc("TRN2", target_bir_lowering=False, num_devices=1)
    t = {k: nc.dram_tensor(f"in_{k}", a.shape, F32, kind="ExternalInput").ap() for k, a in arrays.items()}
    t["out"] = nc.dram_tensor("out", (N, P), F32, kind="ExternalOutput").ap()
    build(nc, t)
    r = run_bass_kernel_spmd(nc, [{f"in_{k}": a for k, a in arrays.items()}], core_ids=[0])
    return r.results[0]["out"]
```

```python
from contextlib import ExitStack

import concourse.bass as bass
import numpy as np
from concourse import mybir

P = 128
N = 2048
HEADS = 3
NB = N // P
RING = 4
BANK = 512
NC = N // BANK
TPC = BANK // P
BPG = 4
MICRO = HEADS * TPC
ASLOT = 2
EARLY = NC - 1
SPLIT = 3
ROWS = 1 + SPLIT * 2 * HEADS
NW = ROWS + 1
ESLOT = 4
BIG = 1e30
ALPHA = 0.2
EPS = 1e-5

ORDER = ["eR", "eH", "eI", "eZ", "nR", "nH", "nI", "nZ", "Ttotal", "Tx1", "Tproj"]
PE_AT = {"eR": 0, "eH": 1, "eI": 2, "eZ": 3, "nR": 4, "nH": 5, "nI": 6, "nZ": 7, "Ttotal": 9, "Tx1": 12, "Tproj": 13}
READ_LAG = 2
GATE_COLS = {"R": 0, "Z": 1, "I": 2, "H": 2}

ALU = mybir.AluOpType
ACT = mybir.ActivationFunctionType
F32 = mybir.dt.float32
BF16 = mybir.dt.bfloat16
I32 = mybir.dt.int32
AX_X = mybir.AxisListType.X


def need(eng, sem, value):
    if isinstance(value, int) and value <= 0:
        return
    eng.wait_ge(sem, value)


def use(c, name):
    return 1 + c * len(ORDER) + ORDER.index(name)


CELL_OPS = 11


def row(ap):
    return ap.rearrange("p o f -> p (o f)")


def build(nc, t):
    with ExitStack() as ctx:
        def sb(name, shape, dt=F32):
            return ctx.enter_context(nc.sbuf_tensor(name, shape, dt))

        def sem(name):
            return ctx.enter_context(nc.semaphore(name))

        ring = sb("ring", [P, RING, N])
        x_nat = sb("x_nat", [P, NB, P])
        xT = sb("xT", [P, N])
        nsT = sb("nsT", [P, N])
        supT = sb("supT", [P, N])
        nscore = sb("nscore", [P, HEADS, N])
        mask = sb("mask", [P, ASLOT, N], BF16)
        att = sb("att", [P, ASLOT, N])
        work = sb("work", [P, (ESLOT + 2) * HEADS * BANK])
        spread_src = sb("spread_src", [P, HEADS, TPC, P])
        scol = sb("scol", [P, NB, 2 * HEADS])
        e_minus = sb("e_minus", [P, HEADS, BANK])
        scratch = sb("scratch", [P, N], BF16)
        minus_n = sb("minus_n", [P, 2, BANK])
        minus = sb("minus", [P, BANK])
        ident = sb("ident", [P, P])
        diag_masks = sb("diag_masks", [P, 2 * NC - 1, P])
        offdiag = diag_masks[:, NC - 1, :]
        ones = diag_masks[:, 0, :]
        gatW = sb("gatW", [P, HEADS, P])
        wih = sb("wih", [P, 2, 3 * P])
        whh = sb("whh", [P, 2, 3 * P])
        bih = sb("bih", [P, 2, 3])
        bhh = sb("bhh", [P, 2, 3])
        gate_b = sb("gate_b", [P, 2, 2])
        l1WT = sb("l1WT", [P, P])
        l1b = sb("l1b", [1, P])
        ones_row = sb("ones_row", [1, P])
        wa = sb("wa", [P, 2, HEADS])
        diag = sb("diag", [P, NB])
        rowsum = sb("rowsum", [P, NB])
        nmin = sb("nmin", [P, HEADS, TPC])
        nmin_set = sb("nmin_set", [P, HEADS, TPC])
        nmin4 = sb("nmin4", [P, NC])
        nmin1 = sb("nmin1", [P, 1])
        neg_count = sb("neg_count", [1, 1])
        neg_flag = sb("neg_flag", [1, 1], I32)
        pause = sb("pause", [P, 1])
        den = sb("den", [P, HEADS, TPC])
        rden = sb("rden", [P, HEADS, TPC])
        g_r = sb("g_r", [P, 2, BANK])
        g_z = sb("g_z", [P, 2, BANK])
        g_h = sb("g_h", [P, 2, BANK])
        g_i = sb("g_i", [P, 2, BANK])
        total = sb("total", [P, BANK])
        x1s = sb("x1s", [P, TPC, P])
        x1T = sb("x1T", [P, BANK])
        stats = sb("stats", [P, TPC, 6])
        mean = sb("mean", [P, TPC])
        spread = sb("spread", [P, TPC])
        powers = sb("powers", [P, 2 * TPC])
        zero_sum = sb("zero_sum", [P, TPC])
        minus_half = sb("minus_half", [P, 2 * TPC])
        r_chunk = sb("r_chunk", [P, TPC])
        r_all = sb("r_all", [P, NB])

        tail = HEADS * BANK
        weights = work[:, 0:ESLOT * tail].rearrange("p (s h c) -> p s h c", s=ESLOT, h=HEADS)
        nmax_row = work[:, ESLOT * tail:(ESLOT + 1) * tail].rearrange("p (h c) -> p h c", h=HEADS)
        rden_row = work[:, (ESLOT + 1) * tail:(ESLOT + 2) * tail].rearrange("p (h c) -> p h c", h=HEADS)
        early = work
        off = [0]

        def carve(words):
            off[0] += words
            return early[:, off[0] - words:off[0]]

        pos = carve(N).bitcast(BF16).rearrange("p (s n) -> p s n", s=2)
        neg = carve(N).bitcast(BF16).rearrange("p (s n) -> p s n", s=2)
        uf = carve(NB * 6).rearrange("p (b c) -> p b c", b=NB)
        upos = carve(NB * NW // 2).bitcast(BF16).rearrange("p (b c) -> p b c", b=NB)
        uneg = carve(NB * NW // 2).bitcast(BF16).rearrange("p (b c) -> p b c", b=NB)
        x_st = carve(RING * P).rearrange("p (s c) -> p s c", s=RING)
        gatWT = carve(HEADS * P).rearrange("p (h c) -> p h c", h=HEADS)
        gata = carve(2 * HEADS).rearrange("p (h c) -> p h c", h=HEADS)
        sum_sel = att[0:ROWS, 0, 0:2 * HEADS]
        spread_sel = carve(HEADS * P)[0:2 * HEADS, :].rearrange("p (c m) -> p c m", c=HEADS)
        score_rows = att[0:ROWS, 1, :]
        rows6 = carve(N)[0:2 * HEADS, :]
        x1 = nsT[:, :].rearrange("p (b f) -> p b f", b=NB)
        gmat = supT[:, :].rearrange("p (b f) -> p b f", b=NB)
        outT = early[:, 0:N]
        x2 = nscore[:, 0, :].rearrange("p (b f) -> p b f", b=NB)
        x2n = nscore[:, 1, :].rearrange("p (b f) -> p b f", b=NB)
        shift = nscore[:, 2, 0:NB]
        stats2 = nscore[:, 2, P:P + 6 * NB].rearrange("p (b c) -> p b c", b=NB)
        mean2, spread2, var2, rstd2 = (nscore[:, 2, 3 * P + NB * k:3 * P + NB * (k + 1)] for k in range(4))

        ps = ctx.enter_context(nc.psum_tensor("ps", [P, 8, BANK], F32))
        ns_bank = ps[:, HEADS, :]
        bcast = ps[:, 4:6, :]
        s_ps = ps[:, 6, :]
        cell = ps[:, 7, :]

        names = """x_in prep_in consts_in load0 load1 load2 load3 wa_mm wa_ready u_mm u_split upos_ready
            diag_zeroed masks_ready x_staged mask_mm_done ns_early rows_out rows_mm rows_neg rows_leaky
            spread_mm nscore_ready  minus_stored minus_in0 minus_in1 flagged
            prep mask_ready rowsum_done paused plus_scored minus_step scored exp_done rden_ready nmin_ready
            group_ready diag_built bcast_mm bcast_out exponent minus_exponent exp_block minus_block minus_weight weighted block_done
            acc_done acc_read ns_ready s_mm s_evac tiny gate_ready const_ready
            cell_mm bank_read cell_vec cand_ready x1_pre x1_stat x1_moment x1_var powers_ready pow_done r_step
            x1_done x1_kept conv_done outT_done out_tr fin_sum x2_pre fin_stat fin_moment fin_step fin_var
            pow2_done fin_shift x2_done stored""".split()
        S = {n: sem(n) for n in names}
        loads = [S[f"load{k}"] for k in range(RING)]
        minus_in = [S["minus_in0"], S["minus_in1"]]

        block = ctx.enter_context(nc.Block())

        prep_loads = [(gatWT, t["gat_WT"].rearrange("h k f -> k h f"))] + [
            (gata[:, h, :], t["gat_aT"][:, h, :]) for h in range(HEADS)] + [(xT[:, :], t["xT"])]
        const_loads = [(sum_sel, t["sum_sel"]), (spread_sel, t["spread_sel"]), (ident[:, :], t["ident"]),
                       (gatW[:, :, :], t["gat_W"].rearrange("h k f -> k h f")),
                       (wih[:, 0, :], t["edge_WihT"]), (wih[:, 1, :], t["node_WihT"]),
                       (whh[:, 0, :], t["edge_WhhT"]), (whh[:, 1, :], t["node_WhhT"]),
                       (bih[:, 0, :], t["edge_bih"]), (bih[:, 1, :], t["node_bih"]),
                       (bhh[:, 0, :], t["edge_bhh"]), (bhh[:, 1, :], t["node_bhh"]),
                       (l1WT[:, :], t["l1WT"]), (l1b[:, :], t["l1b"]), (ones_row[:, :], t["ones_row"]),
                       (diag[:, :], t["adj_diag"])]

        def negatives(eng):
            eng.wait_ge(S["flagged"], 2)
            return eng.value_load(neg_flag[0:1, 0:1], min_val=0, max_val=N)

        @block.sync
        def _(sp):
            def load(slot, src):
                sp.dma_start(ring[:, slot, :], src).then_inc(loads[slot], 16)

            sp.dma_start(diag_masks[:, :, :], t["diag_masks"]).then_inc(S["x_in"], 16)
            sp.dma_start(x_nat[:, :, :], t["x"].rearrange("(b p) f -> p b f", p=P)).then_inc(S["x_in"], 16)
            for k in range(RING):
                load(k, t["adjT"][k * P:(k + 1) * P, :])
            with sp.Fori(1, NB // RING) as it:
                for k in range(RING):
                    sp.wait_ge(S["mask_mm_done"], RING * it - RING + k + 1)
                    load(k, t["adjT"][bass.ds(it * (RING * P) + k * P, P), :])
            def load_tile(i):
                load(i % ASLOT, t["adj"][i * P:(i + 1) * P, :])

            def load_tile_after(it, i):
                sp.wait_ge(S["exp_done"], MICRO * it + HEADS * (i - 1))
                load(i % ASLOT, t["adj"][bass.ds(it * BANK + i * P, P), :])

            def load_group(it, ahead, g):
                slot = ASLOT + g % 2
                sp.dma_start(ring[:, slot, :].rearrange("p (b n) -> p b n", b=BPG),
                             t["adjT"][g * BANK:(g + 1) * BANK, bass.ds(it * BANK + ahead * BANK, BANK)]
                             .rearrange("(b p) n -> p b n", p=P)).then_inc(loads[slot], 16)

            def load_group_after(it, ahead, g):
                sp.wait_ge(S["block_done"], NB * it + NB * ahead + BPG * (g - 1))
                load_group(it, ahead, g)

            def minus_chunks(it, p):
                h = p % HEADS
                q = MICRO * it + p
                for c in range(NC):
                    last = q * (4 * NC + 1) + 4 * (c - 2) + 2 - (1 if c < 2 else 0)
                    need(sp, S["minus_step"], last)
                    sp.dma_start(minus_n[:, c % 2, :], t["minus_rows"][h:h + 1, c * BANK:(c + 1) * BANK]
                                 .broadcast_to([P, BANK])).then_inc(minus_in[c % 2], 16)

            for k in range(ASLOT):
                sp.wait_ge(S["mask_mm_done"], NB - RING + k + 1)
                load_tile(k)
            for g in range(2):
                sp.wait_ge(S["mask_mm_done"], NB - RING + ASLOT + g + 1)
                load_group(0, 0, g)
            sp.wait_ge(S["rows_leaky"], NC)
            sp.dma_start(t["minus_rows"], rows6[HEADS:2 * HEADS, :]).then_inc(S["minus_stored"], 16)

            def first_tiles(signed):
                for p in range(MICRO):
                    if signed:
                        minus_chunks(0, p)
                    if p % HEADS == HEADS - 1:
                        load_tile_after(0, p // HEADS + ASLOT)

            def body(c, signed, tiles, more):
                for j in range(NB):
                    if signed and tiles and j < MICRO:
                        minus_chunks(c, MICRO + j)
                    if j == 3 and tiles:
                        load_tile_after(c, TPC + 2)
                    if j == 4:
                        load_group_after(c, 0, 2)
                    if j == 6 and tiles:
                        load_tile_after(c, TPC + 3)
                    if j == 8:
                        load_group_after(c, 0, 3)
                    if j == 10 and more:
                        load_tile_after(c, 2 * TPC)
                    if j == 12 and more:
                        load_tile_after(c, 2 * TPC + 1)
                    if j == 12 and tiles:
                        load_group_after(c, 1, 0)
                    if j == 15 and tiles:
                        load_group_after(c, 1, 1)

            def middle(signed):
                if signed:
                    sp.wait_ge(S["minus_stored"], 16)
                first_tiles(signed)
                with sp.Fori(0, NC - 2) as it:
                    body(it, signed, True, True)
                body(NC - 2, signed, True, False)
            with sp.If(negatives(sp) > 0):
                middle(True)
            with sp.Else():
                middle(False)
            for k in range(ASLOT):
                sp.wait_ge(S["exp_done"], MICRO * NC)
                load(k, t["adjT"][k * P:(k + 1) * P, :])
            body(NC - 1, False, False, False)
            sp.wait_ge(S["block_done"], NB * NC - BPG)
            load(2, t["adjT"][2 * P:3 * P, :])
            sp.wait_ge(S["weighted"], NB * NC)
            load(3, t["adjT"][3 * P:4 * P, :])
            with sp.Fori(1, NB // RING) as it:
                for k in range(RING):
                    sp.wait_ge(S["conv_done"], RING * it - RING + k + 1)
                    load(k, t["adjT"][bass.ds(it * (RING * P) + k * P, P), :])
            out = t["out"].rearrange("(b p) f -> p b f", p=P)
            for c in range(NC):
                sp.wait_ge(S["x2_done"], TPC * (c + 1))
                sp.dma_start(out[:, TPC * c:TPC * (c + 1), :], x2n[:, TPC * c:TPC * (c + 1), :]).then_inc(S["stored"], 16)
            sp.wait_ge(S["minus_stored"], 16)
            sp.wait_ge(S["stored"], 16 * NC)

        @block.gpsimd
        def _(pool):
            pool.wait_ge(S["x_in"], 32)

            def stage_x(it):
                for k in range(RING):
                    need(pool, S["mask_mm_done"], RING * it - RING + k + 1)
                    nc.gpsimd.tensor_copy(x_st[:, k, :],
                                          row(x_nat[:, bass.ds(RING * it + k, 1), :])).then_inc(S["x_staged"], 1)
            stage_x(0)
            with pool.Fori(1, NB // RING) as it:
                stage_x(it)
            nc.gpsimd.memset(minus_half[:, :], -0.5).then_inc(S["const_ready"], 1)
            pool.wait_ge(S["const_ready"], 1)

            def diagonals(c, values, sem_ready, count, spread):
                pool.wait_ge(sem_ready, count)
                need(pool, S["bcast_mm"], spread)
                nc.gpsimd.tensor_tensor(
                    spread_src[:, :, :, :].rearrange("p h t k -> p (h t) k"),
                    ident[:, :].unsqueeze(1).broadcast_to([P, MICRO, P]),
                    values[:, :, :].rearrange("p h t -> p (h t)").unsqueeze(2).broadcast_to([P, MICRO, P]),
                    ALU.mult).then_inc(S["diag_built"], 1)

            def group(c, g):
                slot = ASLOT + g % 2
                pool.wait_ge(loads[slot], 16 * (NB // RING + 2 * c + g // 2 + 1))
                for b in range(BPG):
                    d = ring[:, slot, b * BANK + b * P:b * BANK + (b + 1) * P]
                    last = nc.gpsimd.tensor_tensor(d, d, row(diag_masks[:, bass.ds(c + NC - 1 - g, 1), :]), ALU.mult)
                last.then_inc(S["group_ready"], 1)

            def power(c):
                pool.wait_ge(S["powers_ready"], c + 1)
                nc.gpsimd.tensor_tensor(powers[:, :], powers[:, :], minus_half[:, :], ALU.pow).then_inc(S["pow_done"], 1)

            def keep(c):
                pool.wait_ge(S["x1_done"], TPC * c + TPC)
                nc.gpsimd.tensor_copy(x1[:, bass.ds(TPC * c, TPC), :], x1s[:, :, :]).then_inc(S["x1_kept"], 1)

            def body(c, first, last_chunk):
                diagonals(c, rden, S["rden_ready"], c + 1, 2 * HEADS * c + HEADS)
                for g in range(1, NC):
                    group(c, g)
                if not last_chunk:
                    diagonals(c + 1, nmin_set, S["nmin_ready"], c + 2, 2 * HEADS * c + 2 * HEADS)
                if not first:
                    power(c - 1)
                if not last_chunk:
                    group(c + 1, 0)
                if not first:
                    keep(c - 1)
            pool.wait_ge(S["consts_in"], 16 * len(const_loads))
            group(0, 0)
            diagonals(0, nmin_set, S["nmin_ready"], 1, 0)
            body(0, True, False)
            with pool.Fori(1, NC - 1) as it:
                body(it, False, False)
            body(NC - 1, False, True)
            power(NC - 1)
            keep(NC - 1)
            for c in range(NC):
                cols = slice(TPC * c, TPC * (c + 1))
                pool.wait_ge(S["fin_var"], c + 1)
                nc.gpsimd.tensor_tensor(rstd2[:, cols], var2[:, cols], minus_half[:, 0:TPC],
                                        ALU.pow).then_inc(S["pow2_done"], 1)

        @block.scalar
        def _(act):
            for dst, src in prep_loads:
                act.dma_start(dst, src).then_inc(S["prep_in"], 16)
            for dst, src in const_loads:
                act.dma_start(dst, src).then_inc(S["consts_in"], 16)
            act.wait_ge(S["wa_mm"], 1)
            nc.scalar.activation(wa[:, :, :], ps[:, 4, 0:6].rearrange("p (h s) -> p s h", s=2),
                                 ACT.Copy).then_inc(S["wa_ready"], 1)
            act.wait_ge(S["mask_mm_done"], NB)
            for c in range(NC):
                nc.scalar.activation(score_rows[:, c * BANK:(c + 1) * BANK], ps[0:ROWS, 4 + c, :],
                                     ACT.Copy).then_inc(S["rows_out"], 1)
            for c in range(NC):
                act.wait_ge(S["rows_mm"], c + 1)
                nc.scalar.activation(rows6[:, c * BANK:(c + 1) * BANK], ps[0:2 * HEADS, 4 + c, :],
                                     ACT.Copy, scale=-1.0).then_inc(S["rows_neg"], 1)
            for h in range(HEADS):
                for c in range(NC):
                    act.wait_ge(S["spread_mm"], NC * h + c + 1)
                    nc.scalar.activation(nscore[:, h, c * BANK:(c + 1) * BANK], ps[:, (NC * h + c) % 8, :],
                                         ACT.Copy).then_inc(S["nscore_ready"], 1)
            act.wait_ge(S["cell_mm"], 1)
            nc.scalar.activation(scol[:, :, :], cell[:, 0:NB * 2 * HEADS].rearrange("p (b r) -> p b r", b=NB),
                                 ACT.Copy, scale=-1.0).then_inc(S["bank_read"], 1)

            def gate_out(c, name):
                k, g = "en".index(name[0]), name[1]
                act.wait_ge(S["cell_mm"], use(c, name) + 1)
                dst, func, bias, scale = {
                    "R": (g_r, ACT.Tanh, gate_b[:, k, 0:1], 0.5), "Z": (g_z, ACT.Tanh, gate_b[:, k, 1:2], 0.5),
                    "H": (g_h, ACT.Identity, bhh[:, k, 2:3], 1.0), "I": (g_i, ACT.Identity, bih[:, k, 2:3], 1.0)}[g]
                nc.scalar.activation(dst[:, k, :], cell, func, bias=bias, scale=scale).then_inc(S["bank_read"], 1)

            def candidate(c, k):
                act.wait_ge(S["cell_vec"], CELL_OPS * c + (2, 7)[k])
                nc.scalar.activation(g_h[:, k, :], g_r[:, k, :], ACT.Tanh).then_inc(S["cand_ready"], 1)

            def x1T_out(c):
                act.wait_ge(S["cell_mm"], use(c, "Tx1") + 1)
                nc.scalar.activation(x1T[:, :], cell, ACT.Copy).then_inc(S["bank_read"], 1)

            def proj_out(c):
                act.wait_ge(S["r_step"], 3 * c + 3)
                act.wait_ge(S["cell_mm"], use(c, "Tproj") + 1)
                for b in range(TPC):
                    last = nc.scalar.activation(row(gmat[:, bass.ds(TPC * c + b, 1), :]), cell[:, b * P:(b + 1) * P],
                                                ACT.Copy, scale=r_chunk[:, b:b + 1])
                last.then_inc(S["bank_read"], 1)

            def row_exp(a, p):
                tile, h = divmod(p, HEADS)
                i, q, rs = TPC * a + tile, MICRO * a + p, tile % ASLOT
                if h == 0:
                    need(act, S["rowsum_done"], i)
                    act.wait_ge(S["prep"], i + 1)
                    nc.scalar.activation(scratch[:, :], ring[:, rs, :], ACT.Copy,
                                         accum_out=rowsum[:, bass.ds(i, 1)]).then_inc(S["rowsum_done"], 1)
                if p == 0:
                    need(act, S["rden_ready"], a)
                act.wait_ge(S["scored"], q + 1)
                nc.scalar.activation(att[:, p % ASLOT, :], att[:, p % ASLOT, :], ACT.Exp, bias=nmin[:, h, tile:tile + 1],
                                     scale=-1.0, accum_out=den[:, h, tile:tile + 1]).then_inc(S["exp_done"], 1)

            def block_exp(c, j):
                b = NB * c + j
                act.wait_ge(S["exponent"], b + 1)
                nc.scalar.activation(weights[:, j % ESLOT, :, :], weights[:, j % ESLOT, :, :],
                                     ACT.Exp).then_inc(S["exp_block"], 1)

            def minus_exp(c, j):
                act.wait_ge(S["minus_exponent"], NB * c + j + 1)
                nc.scalar.activation(e_minus[:, :, :], e_minus[:, :, :], ACT.Exp).then_inc(S["minus_block"], 1)

            def maxima_out(c, heads):
                need(act, S["exponent"], NB * c)
                for h in heads:
                    n = 2 * HEADS * c + h
                    act.wait_ge(S["bcast_mm"], n + 1)
                    nc.scalar.activation(nmax_row[:, h, :], bcast[:, h % 2, :], ACT.Copy).then_inc(S["bcast_out"], 1)

            def denominator_out(c, h):
                n = 2 * HEADS * c + HEADS + h
                need(act, S["s_mm"], HEADS * c)
                act.wait_ge(S["bcast_mm"], n + 1)
                nc.scalar.activation(rden_row[:, h, :], bcast[:, (HEADS + h) % 2, :], ACT.Copy).then_inc(S["bcast_out"], 1)

            def sums_out(c):
                act.wait_ge(S["block_done"], NB * c + NB)
                nc.scalar.activation(nsT[:, bass.ds(c * BANK, BANK)], ns_bank, ACT.Copy).then_inc(S["ns_ready"], 1)

            def support_out(c):
                act.wait_ge(S["s_mm"], HEADS * c + HEADS)
                nc.scalar.activation(supT[:, bass.ds(c * BANK, BANK)], s_ps, ACT.Copy,
                                     scale=1.0 / HEADS).then_inc(S["s_evac"], 1)

            def body(c, signed, first, last_chunk):
                block_exp(c, 0)
                for j in range(NB):
                    if j + 1 < NB:
                        block_exp(c, j + 1)
                    if j == 0 and not first:
                        sums_out(c - 1)
                    if j < MICRO and not last_chunk:
                        row_exp(c + 1, j)
                    if signed:
                        minus_exp(c, j)
                    if j == 2 and not first:
                        support_out(c - 1)
                    if 10 <= j < 10 + HEADS:
                        denominator_out(c, j - 10)
                    if not first:
                        for name in ORDER:
                            if min(PE_AT[name] + READ_LAG, NB - 1) == j and name != "Ttotal":
                                if name[0] != "T":
                                    gate_out(c - 1, name)
                                else:
                                    (x1T_out if name == "Tx1" else proj_out)(c - 1)
                        if j == 5:
                            candidate(c - 1, 0)
                        if j == 9:
                            candidate(c - 1, 1)
                    if j == 14 and not last_chunk and not signed:
                        maxima_out(c + 1, range(0, 2))
                    if j == 15 and not last_chunk:
                        if signed:
                            act.wait_ge(S["minus_exponent"], NB * c + NB)
                        maxima_out(c + 1, range(0 if signed else 2, HEADS))

            def middle(signed):
                for p in range(MICRO):
                    row_exp(0, p)
                maxima_out(0, range(HEADS))
                body(0, signed, True, False)
                with act.Fori(1, NC - 1) as it:
                    body(it, signed, False, False)
                body(NC - 1, signed, False, True)
            act.wait_ge(S["minus_stored"], 16)
            act.wait_ge(S["bank_read"], 1)
            act.wait_ge(S["gate_ready"], 1)
            with act.If(negatives(act) > 0):
                middle(True)
            with act.Else():
                middle(False)
            support_out(NC - 1)
            for name in ORDER:
                if name == "Ttotal":
                    continue
                if name[0] != "T":
                    gate_out(NC - 1, name)
                else:
                    (x1T_out if name == "Tx1" else proj_out)(NC - 1)
                if name == "eI":
                    candidate(NC - 1, 0)
                if name == "nI":
                    candidate(NC - 1, 1)
            act.wait_ge(S["conv_done"], NB)
            for c in range(NC):
                nc.scalar.activation(outT[:, c * BANK:(c + 1) * BANK], ps[:, c, :], ACT.Copy).then_inc(S["outT_done"], 1)
            for c in range(NC):
                act.wait_ge(S["fin_shift"], c + 1)
                for i in range(TPC * c, TPC * (c + 1)):
                    nc.scalar.activation(x2n[:, i, :], x2[:, i, :], ACT.Identity, bias=shift[:, i:i + 1],
                                         scale=rstd2[:, i:i + 1]).then_inc(S["x2_done"], 1)

        @block.vector
        def _(dve):
            V = nc.vector

            def split_projections():
                dve.wait_ge(S["u_mm"], 1)
                V.tensor_copy(uf, ps[:, 5, 0:NB * 6].rearrange("p (b c) -> p b c", b=NB)).then_inc(S["u_split"], 1)
                V.memset(upos[:, :, 0:1], 0.0).then_inc(S["upos_ready"], 1)
                V.memset(uneg[:, :, 0:1], 1.0).then_inc(S["upos_ready"], 1)
                count = 1
                for k in range(SPLIT):
                    dve.wait_ge(S["u_split"], count)
                    part = upos[:, :, 1 + 6 * k:7 + 6 * k]
                    V.tensor_copy(part, uf).then_inc(S["u_split"], 1)
                    count += 1
                    dve.wait_ge(S["u_split"], count)
                    if k < SPLIT - 1:
                        V.tensor_tensor(uf, uf, part, ALU.subtract).then_inc(S["u_split"], 1)
                        count += 1
                    for s in range(2):
                        V.tensor_copy(uneg[:, :, 1 + 6 * k + 3 * s:4 + 6 * k + 3 * s],
                                      upos[:, :, 4 + 6 * k - 3 * s:7 + 6 * k - 3 * s]).then_inc(S["upos_ready"], 1)

            dve.wait_ge(S["x_in"], 32)

            def pass1(it, first):
                for k in range(RING):
                    jb = RING * it + k
                    dve.wait_ge(loads[k], 16 * (it + 1))
                    d = ring[:, k, bass.ds(jb * P, P)]
                    V.tensor_tensor(d, d, offdiag, ALU.mult).then_inc(S["diag_zeroed"], 1)
                    dve.wait_ge(S["diag_zeroed"], jb + 1)
                    need(dve, S["mask_mm_done"], jb - 1)
                    V.tensor_scalar(pos[:, k % 2, :], ring[:, k, :], 0.0, None, ALU.is_gt).then_inc(S["masks_ready"], 1)
                    V.tensor_scalar(neg[:, k % 2, :], ring[:, k, :], 0.0, None, ALU.is_lt).then_inc(S["masks_ready"], 1)
                    if first and k == 0:
                        split_projections()
            pass1(0, True)
            with dve.Fori(1, NB // RING) as it:
                pass1(it, False)
            dve.wait_ge(S["consts_in"], 16 * len(const_loads))
            V.tensor_tensor(gate_b[:, :, :], bih[:, :, 0:2], bhh[:, :, 0:2], ALU.add).then_inc(S["tiny"], 1)
            dve.wait_ge(S["tiny"], 1)
            V.tensor_scalar(gate_b[:, :, :], gate_b[:, :, :], 0.5, None, ALU.mult).then_inc(S["gate_ready"], 1)

            def prepare(a, tile):
                i, rs = TPC * a + tile, tile % ASLOT
                dve.wait_ge(loads[rs], 16 * (NB // RING + 2 * a + tile // ASLOT + 1))
                d = ring[:, rs, bass.ds(i * P, P)]
                V.tensor_tensor(d, d, offdiag, ALU.mult).then_inc(S["prep"], 1)
                if tile >= ASLOT or not (isinstance(a, int) and a == 0):
                    dve.wait_ge(S["scored"], HEADS * (i - 1))
                dve.wait_ge(S["prep"], i + 1)
                V.tensor_scalar(mask[:, rs, :], ring[:, rs, :], 0.0, BIG, ALU.is_le, ALU.mult).then_inc(S["mask_ready"], 1)

            for c in range(NC):
                cols = slice(c * BANK, (c + 1) * BANK)
                dve.wait_ge(S["rows_neg"], c + 1)
                V.scalar_tensor_tensor(out=rows6[:, cols], in0=rows6[:, cols], scalar=ALPHA, in1=rows6[:, cols],
                                       op0=ALU.mult, op1=ALU.min).then_inc(S["rows_leaky"], 1)
            V.tensor_copy(nsT[:, EARLY * BANK:N], ns_bank).then_inc(S["ns_early"], 1)
            V.tensor_reduce(neg_count[:, :], score_rows[0:1, :], AX_X, ALU.max).then_inc(S["flagged"], 1)
            dve.wait_ge(S["flagged"], 1)
            V.tensor_copy(neg_flag[:, :], neg_count[:, :]).then_inc(S["flagged"], 1)

            def score_negative(a, p):
                tile, h = divmod(p, HEADS)
                rs, e, q = tile % ASLOT, p % ASLOT, MICRO * a + p
                done = (4 * NC + 1) * q
                dve.wait_ge(S["plus_scored"], q + 1)
                for c in range(NC):
                    cols = slice(c * BANK, (c + 1) * BANK)
                    need(dve, S["minus_step"], done + 4 * c)
                    V.tensor_scalar(minus[:, :], ring[:, rs, cols], 0.0, BIG, ALU.is_ge,
                                    ALU.mult).then_inc(S["minus_step"], 1)
                    dve.wait_ge(minus_in[c % 2], 16 * (NC // 2 * q + c // 2 + 1))
                    dve.wait_ge(S["minus_step"], done + 4 * c + 1)
                    V.tensor_tensor(minus[:, :], minus[:, :], minus_n[:, c % 2, :], ALU.add).then_inc(S["minus_step"], 1)
                    dve.wait_ge(S["minus_step"], done + 4 * c + 2)
                    V.tensor_reduce(nmin4[:, c:c + 1], minus[:, :], AX_X, ALU.min).then_inc(S["minus_step"], 1)
                    dve.wait_ge(S["minus_step"], done + 4 * c + 3)
                    V.tensor_tensor(att[:, e, cols], att[:, e, cols], minus[:, :], ALU.min).then_inc(S["minus_step"], 1)
                dve.wait_ge(S["minus_step"], done + 4 * NC)
                V.tensor_reduce(nmin1[:, :], nmin4[:, :], AX_X, ALU.min).then_inc(S["minus_step"], 1)
                dve.wait_ge(S["minus_step"], done + 4 * NC + 1)
                V.tensor_tensor(nmin[:, h, tile:tile + 1], nmin[:, h, tile:tile + 1], nmin1[:, :], ALU.min).then_inc(S["scored"], 1)

            def score(a, p, signed):
                tile, h = divmod(p, HEADS)
                rs, e, q, i = tile % ASLOT, p % ASLOT, MICRO * a + p, TPC * a + tile
                if h == 0:
                    prepare(a, tile)
                dve.wait_ge(S["mask_ready"], i + 1)
                if p == 0:
                    need(dve, S["nmin_ready"], a)
                need(dve, S["paused"], q)
                if p >= ASLOT or not (isinstance(a, int) and a == 0):
                    dve.wait_ge(S["exp_done"], q - ASLOT + 1)
                V.memset(pause[:, :], 0.0).then_inc(S["paused"], 1)
                if isinstance(a, int) and a == 0 and tile == 0:
                    dve.wait_ge(S["nscore_ready"], NC * (h + 1))
                V.tensor_tensor_reduce(att[:, e, :], mask[:, rs, :], nscore[:, h, :], 1.0, 3e38, ALU.add, ALU.min,
                                       nmin[:, h, tile:tile + 1]).then_inc(S["plus_scored" if signed else "scored"], 1)
                if signed:
                    score_negative(a, p)

            def set_minima(a):
                dve.wait_ge(S["scored"], MICRO * a + MICRO)
                need(dve, S["diag_built"], 2 * a - 1)
                V.scalar_tensor_tensor(out=nmin_set[:, :, :], in0=nmin[:, :, :], scalar=BIG / 2, in1=nmin[:, :, :],
                                       op0=ALU.is_lt, op1=ALU.mult).then_inc(S["nmin_ready"], 1)

            def reciprocals(a):
                dve.wait_ge(S["exp_done"], MICRO * a + MICRO)
                need(dve, S["diag_built"], 2 * a)
                V.reciprocal(rden[:, :, :], den[:, :, :]).then_inc(S["rden_ready"], 1)

            def exponents(c, j):
                b = NB * c + j
                if j == 0:
                    dve.wait_ge(S["bcast_out"], 2 * HEADS * c + HEADS)
                if j >= ESLOT or not (isinstance(c, int) and c == 0):
                    dve.wait_ge(S["block_done"], b - ESLOT + 1)
                for h in range(HEADS):
                    last = V.tensor_scalar(weights[:, j % ESLOT, h, :], nmax_row[:, h, :], scol[:, j, h:h + 1], 0.0,
                                           ALU.add, ALU.min)
                last.then_inc(S["exponent"], 1)

            def minus_exponents(c, j):
                b = NB * c + j
                if j or not (isinstance(c, int) and c == 0):
                    dve.wait_ge(S["weighted"], b)
                for h in range(HEADS):
                    last = V.tensor_scalar(e_minus[:, h, :], nmax_row[:, h, :], scol[:, j, HEADS + h:HEADS + h + 1],
                                           0.0, ALU.add, ALU.min)
                last.then_inc(S["minus_exponent"], 1)

            def weigh(c, j, signed):
                b = NB * c + j
                slot, e = ASLOT + (j // BPG) % 2, j % ESLOT
                if j % BPG == 0:
                    dve.wait_ge(S["group_ready"], BPG * c + j // BPG + 1)
                adj_block = ring[:, slot, (j % BPG) * BANK:(j % BPG + 1) * BANK]
                dve.wait_ge(S["exp_block"], b + 1)
                if not signed:
                    V.tensor_tensor(weights[:, e, :, :], weights[:, e, :, :],
                                    adj_block.unsqueeze(1).broadcast_to([P, HEADS, BANK]),
                                    ALU.mult).then_inc(S["weighted"], 1)
                    return
                minus_exponents(c, j)
                dve.wait_ge(S["minus_block"], b + 1)
                for h in range(HEADS):
                    done = 2 * (HEADS * b + h)
                    plus, other = weights[:, e, h, :], e_minus[:, h, :]
                    V.scalar_tensor_tensor(out=plus, in0=adj_block, scalar=0.0, in1=plus, op0=ALU.max,
                                           op1=ALU.mult).then_inc(S["minus_weight"], 1)
                    V.scalar_tensor_tensor(out=other, in0=adj_block, scalar=0.0, in1=other, op0=ALU.min,
                                           op1=ALU.mult).then_inc(S["minus_weight"], 1)
                    dve.wait_ge(S["minus_weight"], done + 2)
                    last = V.tensor_tensor(plus, plus, other, ALU.add)
                last.then_inc(S["weighted"], 1)

            def divide(c):
                dve.wait_ge(S["bcast_out"], 2 * HEADS * c + 2 * HEADS)
                for h in range(HEADS):
                    dve.wait_ge(S["acc_done"], HEADS * c + h + 1)
                    V.tensor_tensor(rden_row[:, h, :], ps[:, h, :], rden_row[:, h, :], ALU.mult).then_inc(S["acc_read"], 1)

            def gated(c, k):
                base = CELL_OPS * c + (0, 5)[k]
                dve.wait_ge(S["bank_read"], use(c, ("eI", "nI")[k]) + 1)
                V.scalar_tensor_tensor(out=g_r[:, k, :], in0=g_r[:, k, :], scalar=1.0, in1=g_h[:, k, :], op0=ALU.add,
                                       op1=ALU.mult).then_inc(S["cell_vec"], 1)
                dve.wait_ge(S["cell_vec"], base + 1)
                V.scalar_tensor_tensor(out=g_r[:, k, :], in0=g_r[:, k, :], scalar=0.5, in1=g_i[:, k, :], op0=ALU.mult,
                                       op1=ALU.add).then_inc(S["cell_vec"], 1)

            def mixed(c, k):
                base = CELL_OPS * c + (2, 7)[k]
                dve.wait_ge(S["cand_ready"], 2 * c + k + 1)
                V.tensor_tensor(g_i[:, k, :], xT[:, bass.ds(c * BANK, BANK)], g_h[:, k, :],
                                ALU.subtract).then_inc(S["cell_vec"], 1)
                dve.wait_ge(S["bank_read"], use(c, ("eZ", "nZ")[k]) + 1)
                dve.wait_ge(S["cell_vec"], base + 1)
                V.scalar_tensor_tensor(out=g_i[:, k, :], in0=g_z[:, k, :], scalar=1.0, in1=g_i[:, k, :], op0=ALU.add,
                                       op1=ALU.mult).then_inc(S["cell_vec"], 1)
                dve.wait_ge(S["cell_vec"], base + 2)
                if k == 0:
                    V.scalar_tensor_tensor(out=total[:, :], in0=g_i[:, k, :], scalar=0.5, in1=g_h[:, k, :],
                                           op0=ALU.mult, op1=ALU.add).then_inc(S["cell_vec"], 1)
                    return
                V.scalar_tensor_tensor(out=g_i[:, k, :], in0=g_i[:, k, :], scalar=0.5, in1=g_h[:, k, :], op0=ALU.mult,
                                       op1=ALU.add).then_inc(S["cell_vec"], 1)
                dve.wait_ge(S["cell_vec"], base + 3)
                V.tensor_tensor(total[:, :], total[:, :], g_i[:, k, :], ALU.add).then_inc(S["cell_vec"], 1)

            def residual(c):
                tiles = bass.ds(TPC * c, TPC)
                if isinstance(c, int):
                    dve.wait_ge(S["x1_kept"], c)
                dve.wait_ge(S["cell_mm"], use(c, "Ttotal") + 1)
                for b in range(TPC):
                    V.scalar_tensor_tensor(out=x1s[:, b, :], in0=cell[:, b * P:(b + 1) * P],
                                           scalar=diag[:, bass.ds(TPC * c + b, 1)],
                                           in1=row(x_nat[:, bass.ds(TPC * c + b, 1), :]), op0=ALU.mult,
                                           op1=ALU.add).then_inc(S["bank_read" if b == TPC - 1 else "x1_pre"], 1)
                V.scalar_tensor_tensor(out=powers[:, TPC:2 * TPC], in0=diag[:, tiles], scalar=1.0,
                                       in1=rowsum[:, tiles], op0=ALU.add, op1=ALU.add).then_inc(S["x1_moment"], 1)
                dve.wait_ge(S["x1_pre"], 3 * c + 3)
                dve.wait_ge(S["bank_read"], use(c, "Ttotal") + 1)
                for b in range(TPC):
                    V.bn_stats(stats[:, b, :], x1s[:, b, :]).then_inc(S["x1_stat"], 1)
                base = 6 * c
                dve.wait_ge(S["x1_moment"], base + 1)
                V.tensor_scalar(zero_sum[:, :], powers[:, TPC:2 * TPC], 0.0, None, ALU.is_equal).then_inc(S["x1_moment"], 1)
                dve.wait_ge(S["x1_stat"], TPC * c + TPC)
                V.tensor_tensor(mean[:, :], stats[:, :, 1], stats[:, :, 4], ALU.add).then_inc(S["x1_moment"], 1)
                V.tensor_tensor(spread[:, :], stats[:, :, 1], stats[:, :, 4], ALU.subtract).then_inc(S["x1_moment"], 1)
                dve.wait_ge(S["x1_moment"], base + 4)
                V.tensor_tensor(powers[:, TPC:2 * TPC], powers[:, TPC:2 * TPC], zero_sum[:, :],
                                ALU.add).then_inc(S["x1_moment"], 1)
                variance(mean[:, :], spread[:, :], powers[:, 0:TPC], stats[:, :, 2], stats[:, :, 5], "x1_moment",
                         base + 4, "x1_var", 3 * c, "powers_ready")

            def variance(mean_, spread_, var_, m2a, m2b, moment, base, step, at, done):
                V.tensor_scalar(mean_, mean_, 0.5, None, ALU.mult).then_inc(S[moment], 1)
                V.scalar_tensor_tensor(out=spread_, in0=spread_, scalar=0.25, in1=spread_, op0=ALU.mult,
                                       op1=ALU.mult).then_inc(S[step], 1)
                V.tensor_tensor(var_, m2a, m2b, ALU.add).then_inc(S[step], 1)
                dve.wait_ge(S[step], at + 2)
                V.scalar_tensor_tensor(out=var_, in0=var_, scalar=1.0 / P, in1=spread_, op0=ALU.mult,
                                       op1=ALU.add).then_inc(S[step], 1)
                dve.wait_ge(S[step], at + 3)
                dve.wait_ge(S[moment], base + 2 if moment == "x1_moment" else base + 1)
                V.tensor_scalar(var_, var_, EPS, None, ALU.add).then_inc(S[done], 1)

            def normalise(c):
                dve.wait_ge(S["pow_done"], c + 1)
                for b in range(TPC):
                    V.tensor_scalar(x1s[:, b, :], x1s[:, b, :], mean[:, b:b + 1], powers[:, b:b + 1], ALU.subtract,
                                    ALU.mult).then_inc(S["x1_done"], 1)
                V.tensor_scalar(zero_sum[:, :], zero_sum[:, :], -1.0, 1.0, ALU.mult, ALU.add).then_inc(S["r_step"], 1)
                dve.wait_ge(S["r_step"], 3 * c + 1)
                if not (isinstance(c, int) and c == 0):
                    dve.wait_ge(S["bank_read"], use(c, "Ttotal") + 1)
                V.tensor_tensor(r_chunk[:, :], powers[:, TPC:2 * TPC], zero_sum[:, :], ALU.mult).then_inc(S["r_step"], 1)
                dve.wait_ge(S["r_step"], 3 * c + 2)
                V.tensor_copy(r_all[:, bass.ds(TPC * c, TPC)], r_chunk[:, :]).then_inc(S["r_step"], 1)

            def body(c, signed, first, last_chunk):
                exponents(c, 0)
                exponents(c, 1)
                for j in range(NB):
                    if j < MICRO and not last_chunk:
                        score(c + 1, j, signed)
                    if j == MICRO - 1 and not last_chunk:
                        set_minima(c + 1)
                    weigh(c, j, signed)
                    if j == 0 and not first:
                        divide(c - 1)
                    if j + 2 < NB:
                        exponents(c, j + 2)
                    if j == MICRO + 1 and not last_chunk:
                        reciprocals(c + 1)
                    if first:
                        continue
                    if j == 5:
                        gated(c - 1, 0)
                    if j == 7:
                        mixed(c - 1, 0)
                    if j == 9:
                        gated(c - 1, 1)
                    if j == 10:
                        mixed(c - 1, 1)
                    if j == 12:
                        residual(c - 1)
                    if j == 13:
                        normalise(c - 1)

            def middle(signed):
                for p in range(MICRO):
                    score(0, p, signed)
                set_minima(0)
                reciprocals(0)
                body(0, signed, True, False)
                with dve.Fori(1, NC - 1) as it:
                    body(it, signed, False, False)
                body(NC - 1, signed, False, True)
            with dve.If(negatives(dve) > 0):
                middle(True)
            with dve.Else():
                middle(False)
            divide(NC - 1)
            for k in range(2):
                gated(NC - 1, k)
                mixed(NC - 1, k)
            residual(NC - 1)
            normalise(NC - 1)

            def shift_chunk(c):
                tiles = slice(TPC * c, TPC * (c + 1))
                dve.wait_ge(S["pow2_done"], c + 1)
                V.scalar_tensor_tensor(out=shift[:, tiles], in0=mean2[:, tiles], scalar=-1.0, in1=rstd2[:, tiles],
                                       op0=ALU.mult, op1=ALU.mult).then_inc(S["fin_shift"], 1)

            dve.wait_ge(S["x1_kept"], NC)
            for c in range(NC):
                tiles = slice(TPC * c, TPC * (c + 1))
                xc = x2[:, tiles, :].rearrange("p b f -> p (b f)")
                dve.wait_ge(S["out_tr"], c + 1)
                V.tensor_tensor(xc, ps[:, 4 + c, :], gmat[:, tiles, :].rearrange("p b f -> p (b f)"),
                                ALU.add).then_inc(S["fin_sum"], 1)
                dve.wait_ge(S["fin_sum"], c + 1)
                for i in range(TPC * c, TPC * (c + 1)):
                    V.scalar_tensor_tensor(out=x2[:, i, :], in0=x2[:, i, :], scalar=r_all[:, i:i + 1], in1=x1[:, i, :],
                                           op0=ALU.mult, op1=ALU.add).then_inc(S["x2_pre"], 1)
                for i in range(TPC * c, TPC * (c + 1)):
                    dve.wait_ge(S["x2_pre"], i + 1)
                    V.bn_stats(stats2[:, i, :], x2[:, i, :]).then_inc(S["fin_stat"], 1)
                dve.wait_ge(S["fin_stat"], TPC * (c + 1))
                V.tensor_tensor(mean2[:, tiles], stats2[:, tiles, 1], stats2[:, tiles, 4], ALU.add).then_inc(S["fin_moment"], 1)
                V.tensor_tensor(spread2[:, tiles], stats2[:, tiles, 1], stats2[:, tiles, 4],
                                ALU.subtract).then_inc(S["fin_moment"], 1)
                dve.wait_ge(S["fin_moment"], 3 * c + 2)
                variance(mean2[:, tiles], spread2[:, tiles], var2[:, tiles], stats2[:, tiles, 2], stats2[:, tiles, 5],
                         "fin_moment", 3 * c + 2, "fin_step", 3 * c, "fin_var")
                if c:
                    shift_chunk(c - 1)
            shift_chunk(NC - 1)

        @block.tensor
        def _(pe):
            mm = nc.tensor.matmul

            def projections():
                pe.wait_ge(S["prep_in"], 16 * len(prep_loads))
                for h in range(HEADS):
                    last = mm(ps[:, 4, 2 * h:2 * h + 2], gatWT[:, h, :], gata[:, h, :], start=True, stop=True)
                last.then_inc(S["wa_mm"], 1)
                pe.wait_ge(S["wa_ready"], 1)
                wa_cols = wa[:, :, :].rearrange("p s h -> p (s h)")
                for b in range(NB):
                    last = mm(ps[:, 5, 6 * b:6 * b + 6], xT[:, b * P:(b + 1) * P], wa_cols, start=True, stop=True)
                last.then_inc(S["u_mm"], 1)

            def pass1(it, first):
                for k in range(RING):
                    jb = RING * it + k
                    start = first and k == 0
                    pe.wait_ge(S["x_staged"], jb + 1)
                    pe.wait_ge(S["diag_zeroed"], jb + 1)
                    mm(ns_bank, x_st[:, k, :], ring[:, k, EARLY * BANK:N], start=start, stop=True,
                       skip_group_check=True)
                    if start:
                        projections()
                        pe.wait_ge(S["upos_ready"], 2 * SPLIT + 2)
                    for sgn, (u, m) in enumerate(((upos, pos), (uneg, neg))):
                        pe.wait_ge(S["masks_ready"], 2 * jb + 1 + sgn)
                        for c in range(NC):
                            last = mm(ps[0:ROWS, 4 + c, :], row(u[:, bass.ds(jb, 1), 0:ROWS]),
                                      m[:, k % 2, c * BANK:(c + 1) * BANK], start=start and sgn == 0, stop=True,
                                      skip_group_check=True)
                    last.then_inc(S["mask_mm_done"], 1)
            pass1(0, True)
            with pe.Fori(1, NB // RING) as it:
                pass1(it, False)
            pe.wait_ge(S["consts_in"], 16 * len(const_loads))
            for c in range(NC):
                pe.wait_ge(S["rows_out"], c + 1)
                mm(ps[0:2 * HEADS, 4 + c, :], sum_sel, score_rows[:, c * BANK:(c + 1) * BANK], start=True,
                   stop=True).then_inc(S["rows_mm"], 1)
            pe.wait_ge(S["ns_early"], 1)
            for h in range(HEADS):
                for c in range(NC):
                    n = NC * h + c
                    if h == 0:
                        pe.wait_ge(S["rows_leaky"], c + 1)
                    need(pe, S["nscore_ready"], n - 7)
                    mm(ps[:, n % 8, :], spread_sel[:, h, :], rows6[:, c * BANK:(c + 1) * BANK], start=True,
                       stop=True).then_inc(S["spread_mm"], 1)

            pe.wait_ge(S["nscore_ready"], 8)
            for b in range(NB):
                last = nc.tensor.transpose(cell[:, b * 2 * HEADS:(b + 1) * 2 * HEADS], rows6[:, b * P:(b + 1) * P],
                                           ident[0:2 * HEADS, 0:2 * HEADS])
            last.then_inc(S["cell_mm"], 1)

            def spread(c, k):
                n = 2 * HEADS * c + k
                pe.wait_ge(S["diag_built"], 2 * c + 1 + k // HEADS)
                if k > 1 or not (isinstance(c, int) and c == 0):
                    pe.wait_ge(S["bcast_out"], n - 1)
                mm(bcast[:, k % 2, :], ones, spread_src[:, k % HEADS, :, :].rearrange("p t k -> p (t k)"),
                   start=True, stop=True).then_inc(S["bcast_mm"], 1)

            def product(c, j, sums, first):
                slot, e = ASLOT + (j // BPG) % 2, j % ESLOT
                pe.wait_ge(S["weighted"], NB * c + j + 1)
                for h in range(HEADS):
                    if j == 0 and not first:
                        pe.wait_ge(S["acc_read"], HEADS * (c - 1) + h + 1)
                    last = mm(ps[:, h, :], x_nat[:, j, :], weights[:, e, h, :], start=j == 0, stop=j == NB - 1,
                              skip_group_check=True)
                    if j == NB - 1:
                        last.then_inc(S["acc_done"], 1)
                if not sums:
                    if j < NB - 1:
                        last.then_inc(S["block_done"], 1)
                    return
                if j == 0 and not first:
                    pe.wait_ge(S["ns_ready"], c)
                mm(ns_bank, x_nat[:, j, :], ring[:, slot, (j % BPG) * BANK:(j % BPG + 1) * BANK], start=j == 0,
                   stop=j == NB - 1, skip_group_check=True).then_inc(S["block_done"], 1)

            def project(c):
                for h in range(HEADS):
                    pe.wait_ge(S["acc_read"], HEADS * c + h + 1)
                    mm(s_ps, gatW[:, h, :], rden_row[:, h, :], start=h == 0, stop=h == HEADS - 1,
                       skip_group_check=True).then_inc(S["s_mm"], 1)

            def cell_use(c, name):
                need(pe, S["bank_read"], use(c, name))
                if name[0] != "T":
                    k, g = "en".index(name[0]), name[1]
                    cols = bass.ds(c * BANK, BANK)
                    gate = slice(GATE_COLS[g] * P, (GATE_COLS[g] + 1) * P)
                    if name == "eR" and not (isinstance(c, int) and c == EARLY):
                        pe.wait_ge(S["ns_ready"], c + 1)
                    if name == "nR":
                        pe.wait_ge(S["s_evac"], c + 1)
                    inp = (nsT, supT)[k]
                    if g != "H":
                        last = mm(cell, wih[:, k, gate], inp[:, cols], start=True, stop=g == "I")
                    if g != "I":
                        last = mm(cell, whh[:, k, gate], xT[:, cols], start=g == "H", stop=True)
                elif name == "Ttotal":
                    pe.wait_ge(S["cell_vec"], CELL_OPS * (c + 1))
                    for b in range(TPC):
                        last = nc.tensor.transpose(cell[:, b * P:(b + 1) * P], total[:, b * P:(b + 1) * P], ident[:, :])
                elif name == "Tx1":
                    pe.wait_ge(S["x1_done"], TPC * c + TPC)
                    for b in range(TPC):
                        last = nc.tensor.transpose(cell[:, b * P:(b + 1) * P], x1s[:, b, :], ident[:, :])
                else:
                    for b in range(TPC):
                        mm(cell[:, b * P:(b + 1) * P], x1T[:, b * P:(b + 1) * P], l1WT[:, :], start=True, stop=False,
                           skip_group_check=True)
                        last = mm(cell[:, b * P:(b + 1) * P], ones_row[:, :], l1b[:, :], start=False, stop=True,
                                  skip_group_check=True)
                last.then_inc(S["cell_mm"], 1)

            def body(c, first, last_chunk):
                for j in range(NB):
                    product(c, j, not last_chunk, first)
                    if j == 0 and not first:
                        project(c - 1)
                    if 8 <= j < 8 + HEADS:
                        spread(c, j - 8 + HEADS)
                    if not first:
                        for name in ORDER:
                            if PE_AT[name] == j:
                                cell_use(c - 1, name)
                    if j == 11 and not last_chunk:
                        spread(c + 1, 0)
                        spread(c + 1, 1)
                    if j == 13 and not last_chunk:
                        spread(c + 1, 2)
            pe.wait_ge(S["nscore_ready"], HEADS * NC)
            for k in range(HEADS):
                spread(0, k)
            body(0, True, False)
            with pe.Fori(1, NC - 1) as it:
                body(it, False, False)
            body(NC - 1, False, True)

            beside = {0: ["eR", "eH"], 1: ["eI"], 2: ["eZ"], 3: ["nR"], 4: ["nH"], 5: ["nI"], 6: ["nZ"], 8: ["Ttotal"],
                      10: ["Tx1"], 11: ["Tproj"]}
            pe.wait_ge(S["acc_read"], HEADS * NC)
            pe.wait_ge(S["ns_ready"], NC - 1)
            for jb in range(NB):
                if jb % TPC == 0:
                    pe.wait_ge(S["bank_read"], use(jb // TPC, "Tproj") + 1)
                pe.wait_ge(loads[jb % RING], 16 * (3 * (NB // RING) + jb // RING + 1))
                for c in range(NC):
                    last = mm(ps[:, c, :], gmat[:, jb, :], ring[:, jb % RING, c * BANK:(c + 1) * BANK],
                              start=jb == 0, stop=jb == NB - 1, skip_group_check=True)
                last.then_inc(S["conv_done"], 1)
                if jb == 0:
                    project(NC - 1)
                for name in beside.get(jb, []):
                    cell_use(NC - 1, name)
            for c in range(NC):
                pe.wait_ge(S["outT_done"], c + 1)
                for b in range(TPC):
                    last = nc.tensor.transpose(ps[:, 4 + c, b * P:(b + 1) * P],
                                               outT[:, c * BANK + b * P:c * BANK + (b + 1) * P], ident[:, :])
                last.then_inc(S["out_tr"], 1)


def kernel(x, adj, L0_gnn_gat_W, L0_gnn_gat_a, L0_gnn_edge_Wih, L0_gnn_edge_Whh, L0_gnn_edge_bih, L0_gnn_edge_bhh,
           L0_gnn_node_Wih, L0_gnn_node_Whh, L0_gnn_node_bih, L0_gnn_node_bhh, L1_gnn_W, L1_gnn_b):
    import concourse.bacc as bacc
    from concourse.bass_utils import run_bass_kernel_spmd

    C = np.ascontiguousarray
    adj = np.asarray(adj)
    x = np.asarray(x)
    eye = np.eye(P, dtype=np.float32)
    sum_sel = np.zeros((ROWS, 2 * HEADS), np.float32)
    for r in range(1, ROWS):
        sum_sel[r, (r - 1) % (2 * HEADS)] = 1.0
    spread_sel = np.zeros((2 * HEADS, HEADS, P), np.float32)
    for h in range(HEADS):
        spread_sel[h, h, :] = 1.0
    diag_masks = np.ones((P, 2 * NC - 1, P), np.float32)
    diag_masks[:, NC - 1, :] -= eye
    arrays = {
        "x": C(x), "xT": C(x.T), "adj": C(adj), "adjT": C(adj.T),
        "adj_diag": C(adj.diagonal().reshape(NB, P).T),
        "gat_W": C(L0_gnn_gat_W), "gat_WT": C(np.asarray(L0_gnn_gat_W).transpose(0, 2, 1)),
        "gat_aT": C(np.asarray(L0_gnn_gat_a).reshape(HEADS, 2, P).transpose(2, 0, 1)),
        "edge_WihT": C(np.asarray(L0_gnn_edge_Wih).T), "edge_WhhT": C(np.asarray(L0_gnn_edge_Whh).T),
        "node_WihT": C(np.asarray(L0_gnn_node_Wih).T), "node_WhhT": C(np.asarray(L0_gnn_node_Whh).T),
        "edge_bih": C(np.asarray(L0_gnn_edge_bih).reshape(3, P).T),
        "edge_bhh": C(np.asarray(L0_gnn_edge_bhh).reshape(3, P).T),
        "node_bih": C(np.asarray(L0_gnn_node_bih).reshape(3, P).T),
        "node_bhh": C(np.asarray(L0_gnn_node_bhh).reshape(3, P).T),
        "l1WT": C(np.asarray(L1_gnn_W).T), "l1b": C(np.asarray(L1_gnn_b).reshape(1, P)),
        "ident": eye, "diag_masks": diag_masks, "sum_sel": sum_sel, "spread_sel": spread_sel,
        "ones_row": np.ones((1, P), np.float32),
    }
    nc = bacc.Bacc("TRN2", target_bir_lowering=False, num_devices=1)
    t = {k: nc.dram_tensor(f"in_{k}", a.shape, F32, kind="ExternalInput").ap() for k, a in arrays.items()}
    t["minus_rows"] = nc.dram_tensor("minus_rows", (HEADS, N), F32, kind="Internal").ap()
    t["out"] = nc.dram_tensor("out", (N, P), F32, kind="ExternalOutput").ap()
    build(nc, t)
    r = run_bass_kernel_spmd(nc, [{f"in_{k}": a for k, a in arrays.items()}], core_ids=[0])
    return r.results[0]["out"]
```

```python
from contextlib import ExitStack

import concourse.bass as bass
import numpy as np
from concourse import mybir

P = 128
N = 2048
HEADS = 3
NB = N // P
RING = 4
BANK = 512
NC = N // BANK
TPC = BANK // P
BPG = N // BANK
STEPS = HEADS * TPC
ASLOT = 2
LAST = 3
EARLY = NC - 1
SPLIT = 3
ROWS = 1 + SPLIT * 2 * HEADS
NW = ROWS + 1
ESLOT = 4
BIG = 1e30
ALPHA = 0.2
EPS = 1e-5

ORDER = ["eR", "eH", "eI", "eZ", "nR", "nH", "nI", "nZ", "Ttotal", "Tx1", "Tproj"]
PE_AT = {"eR": 0, "eH": 1, "eI": 2, "eZ": 3, "nR": 4, "nH": 5, "nI": 6, "nZ": 7, "Ttotal": 9, "Tx1": 12, "Tproj": 13}
READ_LAG = 2
GATE_COLS = {"R": 0, "Z": 1, "I": 2, "H": 2}

ALU = mybir.AluOpType
ACT = mybir.ActivationFunctionType
F32 = mybir.dt.float32
BF16 = mybir.dt.bfloat16
I32 = mybir.dt.int32
AX_X = mybir.AxisListType.X


def need(eng, sem, value):
    if isinstance(value, int) and value <= 0:
        return
    eng.wait_ge(sem, value)


def use(c, name):
    return 1 + c * len(ORDER) + ORDER.index(name)


SPREAD_BANKS = [[0, 1, 2, 4], [5, 6, 7, 3], [0, 1, 2, 4]]
BODY_BANKS = [4, 5, 6, 4, 5, 4]
MINUS_BANKS = [5, 6, 7, 3]


def tile_head(a, p):
    if isinstance(a, int) and a == 0 and p < ASLOT * HEADS:
        return p % ASLOT, p // ASLOT
    return divmod(p, HEADS)


def tile_slot(a, tile):
    return tile if isinstance(a, int) and a == 0 else tile % ASLOT


def tile_loads(a, tile):
    if isinstance(a, int) and a == 0:
        return NB // RING + 1
    return 2 * a + (NB // RING + tile // ASLOT)


def before_conv(slot):
    return NB // RING + 1 + (2 * (NC - 1) if slot < ASLOT else 2 * NC)


def last_step(tile):
    return max(p for p in range(STEPS) if tile_head(0, p)[0] == tile)


def vector_heads(j):
    return HEADS - 1 if j % 3 else HEADS - 2


CELL_OPS = 11


def row(ap):
    return ap.rearrange("p o f -> p (o f)")


def build(nc, t):
    with ExitStack() as ctx:
        def sb(name, shape, dt=F32):
            return ctx.enter_context(nc.sbuf_tensor(name, shape, dt))

        def sem(name):
            return ctx.enter_context(nc.semaphore(name))

        ring = sb("ring", [P, RING, N])
        x_nat = sb("x_nat", [P, NB, P])
        xT = sb("xT", [P, N])
        nsT = sb("nsT", [P, N])
        supT = sb("supT", [P, N])
        nscore = sb("nscore", [P, HEADS, N])
        mask = sb("mask", [P, ASLOT, N], BF16)
        att = sb("att", [P, ASLOT, N])
        work = sb("work", [P, (ESLOT + 2) * HEADS * BANK])
        spread_src = sb("spread_src", [P, HEADS, TPC, P])
        scol = sb("scol", [P, NB, 2 * HEADS])
        e_minus = sb("e_minus", [P, HEADS, BANK])
        scratch = sb("scratch", [P, N], BF16)
        minus_n = sb("minus_n", [P, 2, BANK])
        minus = sb("minus", [P, BANK])
        ident = sb("ident", [P, P])
        diag_masks = sb("diag_masks", [P, 2 * NC - 1, P])
        offdiag = diag_masks[:, NC - 1, :]
        ones = diag_masks[:, 0, :]
        gatW = sb("gatW", [P, HEADS, P])
        wih = sb("wih", [P, 2, 3 * P])
        whh = sb("whh", [P, 2, 3 * P])
        bih = sb("bih", [P, 2, 3])
        bhh = sb("bhh", [P, 2, 3])
        gate_b = sb("gate_b", [P, 2, 2])
        l1WT = sb("l1WT", [P, P])
        l1b = sb("l1b", [1, P])
        ones_row = sb("ones_row", [1, P])
        wa = sb("wa", [P, 2, HEADS])
        diag = sb("diag", [P, NB])
        rowsum = sb("rowsum", [P, NB])
        nmin = sb("nmin", [P, HEADS, TPC])
        nmin_set = sb("nmin_set", [P, HEADS, TPC])
        nmin4 = sb("nmin4", [P, NC])
        nmin1 = sb("nmin1", [P, 1])
        row_sums = sb("row_sums", [ROWS, NC])
        neg_count = sb("neg_count", [1, 1])
        neg_flag = sb("neg_flag", [1, 1], I32)
        pause = sb("pause", [P, 1])
        den = sb("den", [P, HEADS, TPC])
        rden = sb("rden", [P, HEADS, TPC])
        g_r = sb("g_r", [P, 2, BANK])
        g_z = sb("g_z", [P, 2, BANK])
        g_h = sb("g_h", [P, 2, BANK])
        g_i = sb("g_i", [P, 2, BANK])
        total = sb("total", [P, BANK])
        x1s = sb("x1s", [P, TPC, P])
        x1T = sb("x1T", [P, BANK])
        stats = sb("stats", [P, TPC, 6])
        mean = sb("mean", [P, TPC])
        spread = sb("spread", [P, TPC])
        powers = sb("powers", [P, 2 * TPC])
        zero_sum = sb("zero_sum", [P, TPC])
        minus_half = sb("minus_half", [P, 2 * TPC])
        r_chunk = sb("r_chunk", [P, TPC])
        r_all = sb("r_all", [P, NB])

        per_block = HEADS * BANK
        weights = work[:, 0:ESLOT * per_block].rearrange("p (s h c) -> p s h c", s=ESLOT, h=HEADS)
        max_row = work[:, ESLOT * per_block:(ESLOT + 1) * per_block].rearrange("p (h c) -> p h c", h=HEADS)
        rden_row = work[:, (ESLOT + 1) * per_block:(ESLOT + 2) * per_block].rearrange("p (h c) -> p h c", h=HEADS)
        off = [0]

        def carve(words):
            off[0] += words
            return work[:, off[0] - words:off[0]]

        pos = carve(N).bitcast(BF16).rearrange("p (s n) -> p s n", s=2)
        neg = carve(N).bitcast(BF16).rearrange("p (s n) -> p s n", s=2)
        uf = carve(NB * 6).rearrange("p (b c) -> p b c", b=NB)
        upos = carve(NB * NW // 2).bitcast(BF16).rearrange("p (b c) -> p b c", b=NB)
        uneg = carve(NB * NW // 2).bitcast(BF16).rearrange("p (b c) -> p b c", b=NB)
        x_st = carve(RING * P).rearrange("p (s c) -> p s c", s=RING)
        gatWT = carve(HEADS * P).rearrange("p (h c) -> p h c", h=HEADS)
        gata = carve(2 * HEADS).rearrange("p (h c) -> p h c", h=HEADS)
        sum_sel = carve(2 * HEADS)[0:ROWS, :]
        spread_sel = carve(HEADS * P)[0:ROWS, :].rearrange("p (c m) -> p c m", c=HEADS)
        score_rows = carve(N)[0:ROWS, :]
        minus_rows = work[0:HEADS, 0:N]
        x1 = nsT[:, :].rearrange("p (b f) -> p b f", b=NB)
        gmat = supT[:, :].rearrange("p (b f) -> p b f", b=NB)
        outT = work[:, 0:N]
        x2 = nscore[:, 0, :].rearrange("p (b f) -> p b f", b=NB)
        x2n = nscore[:, 1, :].rearrange("p (b f) -> p b f", b=NB)
        shift = nscore[:, 2, 0:NB]
        stats2 = nscore[:, 2, P:P + 6 * NB].rearrange("p (b c) -> p b c", b=NB)
        mean2, spread2, var2, rstd2 = (nscore[:, 2, 3 * P + NB * k:3 * P + NB * (k + 1)] for k in range(4))

        ps = ctx.enter_context(nc.psum_tensor("ps", [P, 8, BANK], F32))
        ns_bank = ps[:, HEADS, :]
        s_ps = ps[:, 6, :]
        cell = ps[:, 7, :]

        names = """x_in offdiag_in prep_in consts_in late_in load0 load1 load2 load3 wa_mm wa_ready u_mm u_split
            upos_ready
            diag_zeroed masks_ready x_staged mask_mm_done ns_early rows_out
            spread_mm nscore_ready scaled minus_mm minus_out minus_stored minus_in0 minus_in1 flagged
            prep mask_ready rowsum_done paused plus_scored minus_step scored exp_done rden_ready nmin_ready
            group_ready diag_built bcast_mm bcast_out depth other_depth minus_depth exp_block
            minus_block minus_weight weighted block_done
            acc_done acc_read ns_ready s_mm s_evac gate_sum gate_ready const_ready
            cell_mm bank_read cell_vec cand_ready x1_pre x1_stat x1_moment x1_var powers_ready pow_done r_step
            x1_done x1_kept conv_done conv_out outT_done out_tr fin_sum x2_pre fin_stat fin_moment fin_step fin_var
            pow2_done fin_shift x2_done stored""".split()
        S = {n: sem(n) for n in names}
        loads = [S[f"load{k}"] for k in range(RING)]
        minus_in = [S["minus_in0"], S["minus_in1"]]

        block = ctx.enter_context(nc.Block())

        prep_loads = [(gatWT, t["gat_WT"].rearrange("h k f -> k h f")), (gata, t["gat_aT"]), (xT[:, :], t["xT"])]
        const_loads = [(sum_sel, t["sum_sel"]), (spread_sel, t["spread_sel"])]
        late_loads = [(diag_masks[:, 0:NC - 1, :], t["diag_masks"][:, 0:NC - 1, :]), (ident[:, :], t["ident"]),
                      (gatW[:, :, :], t["gat_W"].rearrange("h k f -> k h f")),
                      (wih[:, 0, :], t["edge_WihT"]), (wih[:, 1, :], t["node_WihT"]),
                      (whh[:, 0, :], t["edge_WhhT"]), (whh[:, 1, :], t["node_WhhT"]),
                      (bih[:, 0, :], t["edge_bih"]), (bih[:, 1, :], t["node_bih"]),
                      (bhh[:, 0, :], t["edge_bhh"]), (bhh[:, 1, :], t["node_bhh"]),
                      (l1WT[:, :], t["l1WT"]), (l1b[:, :], t["l1b"]), (ones_row[:, :], t["ones_row"]),
                      (diag[:, :], t["adj_diag"]),
                      (diag_masks[:, NC:2 * NC - 1, :], t["diag_masks"][:, NC:2 * NC - 1, :])]

        def negatives(eng):
            eng.wait_ge(S["flagged"], 2)
            return eng.value_load(neg_flag[0:1, 0:1], min_val=0, max_val=N * N)

        @block.sync
        def _(sp):
            def load(slot, src):
                sp.dma_start(ring[:, slot, :], src).then_inc(loads[slot], 16)

            for dst, src in prep_loads:
                sp.dma_start(dst, src).then_inc(S["prep_in"], 16)
            sp.dma_start(offdiag, t["diag_masks"][:, NC - 1, :]).then_inc(S["offdiag_in"], 16)
            load(0, t["adjT"][0:P, :])
            sp.dma_start(x_nat[:, :, :], t["x"].rearrange("(b p) f -> p b f", p=P)).then_inc(S["x_in"], 16)
            for k in range(1, RING):
                load(k, t["adjT"][k * P:(k + 1) * P, :])
            with sp.Fori(1, NB // RING) as it:
                for k in range(RING):
                    sp.wait_ge(S["mask_mm_done"], RING * it - RING + k + 1)
                    load(k, t["adjT"][bass.ds(it * (RING * P) + k * P, P), :])

            def load_tile(i):
                load(i % ASLOT, t["adj"][i * P:(i + 1) * P, :])

            def load_tile_after(it, i):
                sp.wait_ge(S["exp_done"], STEPS * it + HEADS * (i - 1))
                load(i % ASLOT, t["adj"][bass.ds(it * BANK + i * P, P), :])

            def load_group(it, ahead, g):
                slot = ASLOT + g % 2
                sp.dma_start(ring[:, slot, :].rearrange("p (b n) -> p b n", b=BPG),
                             t["adjT"][g * BANK:(g + 1) * BANK, bass.ds(it * BANK + ahead * BANK, BANK)]
                             .rearrange("(b p) n -> p b n", p=P)).then_inc(loads[slot], 16)

            def load_group_after(it, ahead, g):
                sp.wait_ge(S["block_done"], NB * it + NB * ahead + BPG * (g - 1))
                load_group(it, ahead, g)

            def minus_chunks(it, p):
                h = tile_head(it, p)[1]
                q = STEPS * it + p
                for c in range(NC):
                    last = q * (5 * NC + 1) + 5 * (c - 2) + 3 - (1 if c < 2 else 0)
                    need(sp, S["minus_step"], last)
                    sp.dma_start(minus_n[:, c % 2, :], t["minus_rows"][h:h + 1, c * BANK:(c + 1) * BANK]
                                 .broadcast_to([P, BANK])).then_inc(minus_in[c % 2], 16)

            for k in range(RING):
                sp.wait_ge(S["mask_mm_done"], NB - RING + k + 1)
                load(k, t["adj"][k * P:(k + 1) * P, :])
            for dst, src in late_loads:
                sp.dma_start(dst, src).then_inc(S["late_in"], 16)
            sp.wait_ge(S["minus_out"], NC)
            sp.dma_start(t["minus_rows"], minus_rows).then_inc(S["minus_stored"], 16)

            def first_tiles(signed):
                for p in range(STEPS):
                    if signed:
                        minus_chunks(0, p)
                    for k in range(ASLOT):
                        if p == last_step(k):
                            sp.wait_ge(S["exp_done"], p + 1)
                            load_tile(TPC + k)
                        if p == HEADS * (ASLOT + k + 1) - 1:
                            sp.wait_ge(S["exp_done"], p + 1)
                            load_group(0, 0, k)

            def body(c, signed, tiles, more):
                for j in range(NB):
                    if signed and tiles and j < STEPS:
                        minus_chunks(c, STEPS + j)
                    if j == 3 and tiles:
                        load_tile_after(c, TPC + 2)
                    if j == 4:
                        load_group_after(c, 0, 2)
                    if j == 6 and tiles:
                        load_tile_after(c, TPC + 3)
                    if j == 8:
                        load_group_after(c, 0, 3)
                    if j == 10 and more:
                        load_tile_after(c, 2 * TPC)
                    if j == 12 and more:
                        load_tile_after(c, 2 * TPC + 1)
                    if j == 12 and tiles:
                        load_group_after(c, 1, 0)
                    if j == 15 and tiles:
                        load_group_after(c, 1, 1)

            def middle(signed):
                if signed:
                    sp.wait_ge(S["minus_stored"], 16)
                first_tiles(signed)
                with sp.Fori(0, NC - 2) as it:
                    body(it, signed, True, True)
                body(NC - 2, signed, True, False)
            with sp.If(negatives(sp) > 0):
                middle(True)
            with sp.Else():
                middle(False)
            for k in range(ASLOT):
                sp.wait_ge(S["exp_done"], STEPS * NC)
                load(k, t["adjT"][k * P:(k + 1) * P, :])
            body(NC - 1, False, False, False)
            sp.wait_ge(S["block_done"], NB * NC - BPG)
            load(2, t["adjT"][2 * P:3 * P, :])
            sp.wait_ge(S["weighted"], NB * NC)
            load(3, t["adjT"][3 * P:4 * P, :])
            with sp.Fori(1, NB // RING) as it:
                for k in range(RING):
                    sp.wait_ge(S["conv_done"], RING * it - RING + k + 1)
                    load(k, t["adjT"][bass.ds(it * (RING * P) + k * P, P), :])
            out = t["out"].rearrange("(b p) f -> p b f", p=P)
            for c in range(NC):
                sp.wait_ge(S["x2_done"], TPC * (c + 1))
                sp.dma_start(out[:, TPC * c:TPC * (c + 1), :], x2n[:, TPC * c:TPC * (c + 1), :]).then_inc(S["stored"], 16)
            sp.wait_ge(S["minus_stored"], 16)
            sp.wait_ge(S["stored"], 16 * NC)

        @block.gpsimd
        def _(pool):
            pool.wait_ge(S["x_in"], 16)

            def stage_x(it):
                for k in range(RING):
                    need(pool, S["mask_mm_done"], RING * it - RING + k + 1)
                    nc.gpsimd.tensor_copy(x_st[:, k, :],
                                          row(x_nat[:, bass.ds(RING * it + k, 1), :])).then_inc(S["x_staged"], 1)
            stage_x(0)
            with pool.Fori(1, NB // RING) as it:
                stage_x(it)
            nc.gpsimd.memset(minus_half[:, :], -0.5).then_inc(S["const_ready"], 1)
            pool.wait_ge(S["const_ready"], 1)

            def diagonals(c, values, sem_ready, count, spread, tiles=slice(0, TPC)):
                n = tiles.stop - tiles.start
                pool.wait_ge(sem_ready, count)
                need(pool, S["bcast_mm"], spread)
                nc.gpsimd.tensor_tensor(
                    spread_src[:, :, tiles, :],
                    ident[:, :].unsqueeze(1).unsqueeze(1).broadcast_to([P, HEADS, n, P]),
                    values[:, :, tiles].unsqueeze(3).broadcast_to([P, HEADS, n, P]),
                    ALU.mult).then_inc(S["diag_built"], 1)

            def group(c, g):
                slot = ASLOT + g % 2
                pool.wait_ge(loads[slot], 32 * c + 16 * (NB // RING + 1 + g // 2 + 1))
                for b in range(BPG):
                    d = ring[:, slot, b * BANK + b * P:b * BANK + (b + 1) * P]
                    last = nc.gpsimd.tensor_tensor(d, d, row(diag_masks[:, bass.ds(c + NC - 1 - g, 1), :]), ALU.mult)
                last.then_inc(S["group_ready"], 1)

            def power(c):
                pool.wait_ge(S["powers_ready"], c + 1)
                nc.gpsimd.tensor_tensor(powers[:, :], powers[:, :], minus_half[:, :], ALU.pow).then_inc(S["pow_done"], 1)

            def keep(c):
                pool.wait_ge(S["x1_done"], TPC * c + TPC)
                nc.gpsimd.tensor_copy(x1[:, bass.ds(TPC * c, TPC), :], x1s[:, :, :]).then_inc(S["x1_kept"], 1)

            def body(c, first, last_chunk):
                diagonals(c, rden, S["rden_ready"], c + 1, 2 * HEADS * c + HEADS)
                for g in range(1, NC):
                    group(c, g)
                if not last_chunk:
                    diagonals(c + 1, nmin_set, S["nmin_ready"], TPC + c + 1, 2 * HEADS * c + 2 * HEADS)
                if not first:
                    power(c - 1)
                if not last_chunk:
                    group(c + 1, 0)
                if not first:
                    keep(c - 1)
            pool.wait_ge(S["late_in"], 16 * len(late_loads))
            group(0, 0)
            for k in range(TPC):
                diagonals(0, nmin_set, S["nmin_ready"], k + 1, 0, slice(k, k + 1))
            body(0, True, False)
            with pool.Fori(1, NC - 1) as it:
                body(it, False, False)
            body(NC - 1, False, True)
            power(NC - 1)
            keep(NC - 1)
            for c in range(NC):
                cols = slice(TPC * c, TPC * (c + 1))
                pool.wait_ge(S["fin_var"], c + 1)
                nc.gpsimd.tensor_tensor(rstd2[:, cols], var2[:, cols], minus_half[:, 0:TPC],
                                        ALU.pow).then_inc(S["pow2_done"], 1)

        @block.scalar
        def _(act):
            act.wait_ge(S["wa_mm"], 1)
            nc.scalar.activation(wa[:, :, :], ps[:, 4, 0:6].rearrange("p (h s) -> p s h", s=2),
                                 ACT.Copy).then_inc(S["wa_ready"], 1)
            for dst, src in const_loads:
                act.dma_start(dst, src).then_inc(S["consts_in"], 16)
            act.wait_ge(S["mask_mm_done"], NB)
            for c in range(NC):
                nc.scalar.activation(score_rows[:, c * BANK:(c + 1) * BANK], ps[0:ROWS, 4 + c, :], ACT.Copy,
                                     accum_out=row_sums[:, c:c + 1]).then_inc(S["rows_out"], 1)
            nc.scalar.activation(nsT[:, EARLY * BANK:N], ns_bank, ACT.Copy).then_inc(S["ns_early"], 1)

            def minus_rows_out():
                for c in range(NC):
                    act.wait_ge(S["minus_mm"], c + 1)
                    nc.scalar.activation(minus_rows[:, c * BANK:(c + 1) * BANK], ps[0:HEADS, MINUS_BANKS[c], :],
                                         ACT.Copy).then_inc(S["minus_out"], 1)

            def scale_scores(h):
                for c in range(NC):
                    act.wait_ge(S["spread_mm"], NC * h + c + 1)
                    nc.scalar.activation(nscore[:, h, c * BANK:(c + 1) * BANK], ps[:, SPREAD_BANKS[h][c], :], ACT.Copy,
                                         scale=ALPHA).then_inc(S["scaled"], 1)

            def scale_columns():
                act.wait_ge(S["cell_mm"], 1)
                nc.scalar.activation(scol[:, :, :], cell[:, 0:NB * 2 * HEADS].rearrange("p (b r) -> p b r", b=NB),
                                     ACT.Copy, scale=ALPHA).then_inc(S["scaled"], 1)

            def gate_out(c, name):
                k, g = "en".index(name[0]), name[1]
                act.wait_ge(S["cell_mm"], use(c, name) + 1)
                dst, func, bias, scale = {
                    "R": (g_r, ACT.Tanh, gate_b[:, k, 0:1], 0.5), "Z": (g_z, ACT.Tanh, gate_b[:, k, 1:2], 0.5),
                    "H": (g_h, ACT.Identity, bhh[:, k, 2:3], 1.0), "I": (g_i, ACT.Identity, bih[:, k, 2:3], 1.0)}[g]
                nc.scalar.activation(dst[:, k, :], cell, func, bias=bias, scale=scale).then_inc(S["bank_read"], 1)

            def candidate(c, k):
                act.wait_ge(S["cell_vec"], CELL_OPS * c + (2, 7)[k])
                nc.scalar.activation(g_h[:, k, :], g_r[:, k, :], ACT.Tanh).then_inc(S["cand_ready"], 1)

            def x1T_out(c):
                act.wait_ge(S["cell_mm"], use(c, "Tx1") + 1)
                nc.scalar.activation(x1T[:, :], cell, ACT.Copy).then_inc(S["bank_read"], 1)

            def proj_out(c):
                act.wait_ge(S["r_step"], 3 * c + 3)
                act.wait_ge(S["cell_mm"], use(c, "Tproj") + 1)
                for b in range(TPC):
                    last = nc.scalar.activation(row(gmat[:, bass.ds(TPC * c + b, 1), :]), cell[:, b * P:(b + 1) * P],
                                                ACT.Copy, scale=r_chunk[:, b:b + 1])
                last.then_inc(S["bank_read"], 1)

            def row_exp(a, p):
                tile, h = tile_head(a, p)
                i, q, rs = TPC * a + tile, STEPS * a + p, tile_slot(a, tile)
                if h == 0:
                    need(act, S["rowsum_done"], i)
                    act.wait_ge(S["prep"], i + 1)
                    nc.scalar.activation(scratch[:, :], ring[:, rs, :], ACT.Copy,
                                         accum_out=rowsum[:, bass.ds(i, 1)]).then_inc(S["rowsum_done"], 1)
                if p == 0:
                    need(act, S["rden_ready"], a)
                act.wait_ge(S["scored"], q + 1)
                nc.scalar.activation(att[:, p % ASLOT, :], att[:, p % ASLOT, :], ACT.Exp, bias=nmin[:, h, tile:tile + 1],
                                     scale=-1.0, accum_out=den[:, h, tile:tile + 1]).then_inc(S["exp_done"], 1)

            def other_depths(c, j):
                if j == 0:
                    act.wait_ge(S["bcast_out"], 2 * HEADS * c + HEADS)
                if j >= ESLOT or not (isinstance(c, int) and c == 0):
                    act.wait_ge(S["block_done"], NB * c + j - ESLOT + 1)
                for h in range(vector_heads(j), HEADS):
                    last = nc.scalar.activation(weights[:, j % ESLOT, h, :], max_row[:, h, :], ACT.Relu,
                                                bias=scol[:, j, h:h + 1])
                last.then_inc(S["other_depth"], 1)

            def block_exp(c, j):
                b = NB * c + j
                act.wait_ge(S["depth"], b + 1)
                act.wait_ge(S["other_depth"], b + 1)
                nc.scalar.activation(weights[:, j % ESLOT, :, :], weights[:, j % ESLOT, :, :], ACT.Exp,
                                     scale=-1.0).then_inc(S["exp_block"], 1)

            def minus_exp(c, j):
                act.wait_ge(S["minus_depth"], NB * c + j + 1)
                nc.scalar.activation(e_minus[:, :, :], e_minus[:, :, :], ACT.Exp,
                                     scale=-1.0).then_inc(S["minus_block"], 1)

            def maxima_out(c):
                need(act, S["depth"], NB * c)
                need(act, S["other_depth"], NB * c)
                for h in range(HEADS):
                    n = 2 * HEADS * c + h
                    act.wait_ge(S["bcast_mm"], n + 1)
                    nc.scalar.activation(max_row[:, h, :], ps[:, BODY_BANKS[h], :], ACT.Copy,
                                         scale=-1.0).then_inc(S["bcast_out"], 1)

            def denominator_out(c, h):
                n = 2 * HEADS * c + HEADS + h
                need(act, S["s_mm"], HEADS * c)
                act.wait_ge(S["bcast_mm"], n + 1)
                nc.scalar.activation(rden_row[:, h, :], ps[:, BODY_BANKS[HEADS + h], :],
                                     ACT.Copy).then_inc(S["bcast_out"], 1)

            def sums_out(c):
                act.wait_ge(S["block_done"], NB * c + NB)
                nc.scalar.activation(nsT[:, bass.ds(c * BANK, BANK)], ns_bank, ACT.Copy).then_inc(S["ns_ready"], 1)

            def support_out(c):
                act.wait_ge(S["s_mm"], HEADS * c + HEADS)
                nc.scalar.activation(supT[:, bass.ds(c * BANK, BANK)], s_ps, ACT.Copy,
                                     scale=1.0 / HEADS).then_inc(S["s_evac"], 1)

            def body(c, signed, first, last_chunk):
                other_depths(c, 0)
                other_depths(c, 1)
                block_exp(c, 0)
                for j in range(NB):
                    if j + 1 < NB:
                        block_exp(c, j + 1)
                    if j == 0 and not first:
                        sums_out(c - 1)
                    if j < STEPS and not last_chunk:
                        row_exp(c + 1, j)
                    if signed:
                        minus_exp(c, j)
                    if j + 2 < NB:
                        other_depths(c, j + 2)
                    if j == 2 and not first:
                        support_out(c - 1)
                    if 10 <= j < 10 + HEADS:
                        denominator_out(c, j - 10)
                    if not first:
                        for name in ORDER:
                            if min(PE_AT[name] + READ_LAG, NB - 1) == j and name != "Ttotal":
                                if name[0] != "T":
                                    gate_out(c - 1, name)
                                else:
                                    (x1T_out if name == "Tx1" else proj_out)(c - 1)
                        if j == 5:
                            candidate(c - 1, 0)
                        if j == 9:
                            candidate(c - 1, 1)
                    if j == (15 if signed else 14) and not last_chunk:
                        if signed:
                            act.wait_ge(S["minus_depth"], NB * c + NB)
                        maxima_out(c + 1)

            def middle(signed):
                scale_scores(0)
                if signed:
                    scale_scores(1)
                    scale_scores(2)
                    minus_rows_out()
                for p in range(STEPS):
                    if not signed and p in (1, 3):
                        scale_scores(p // 2 + 1)
                    if not signed and p == 5:
                        minus_rows_out()
                    if p == 9:
                        scale_columns()
                    row_exp(0, p)
                maxima_out(0)
                act.wait_ge(S["bank_read"], 1)
                act.wait_ge(S["gate_ready"], 1)
                act.wait_ge(S["minus_stored"], 16)
                body(0, signed, True, False)
                with act.Fori(1, NC - 1) as it:
                    body(it, signed, False, False)
                body(NC - 1, signed, False, True)
            act.wait_ge(S["ns_early"], 1)
            with act.If(negatives(act) > 0):
                middle(True)
            with act.Else():
                middle(False)
            support_out(NC - 1)
            for name in ORDER:
                if name == "Ttotal":
                    continue
                if name[0] != "T":
                    gate_out(NC - 1, name)
                else:
                    (x1T_out if name == "Tx1" else proj_out)(NC - 1)
                if name == "eI":
                    candidate(NC - 1, 0)
                if name == "nI":
                    candidate(NC - 1, 1)
            for c in range(NC):
                act.wait_ge(S["conv_out"], c + 1)
                nc.scalar.activation(outT[:, c * BANK:(c + 1) * BANK], ps[:, c, :], ACT.Copy).then_inc(S["outT_done"], 1)
            for c in range(NC):
                act.wait_ge(S["fin_shift"], c + 1)
                for i in range(TPC * c, TPC * (c + 1)):
                    nc.scalar.activation(x2n[:, i, :], x2[:, i, :], ACT.Identity, bias=shift[:, i:i + 1],
                                         scale=rstd2[:, i:i + 1]).then_inc(S["x2_done"], 1)

        @block.vector
        def _(dve):
            V = nc.vector

            def split_projections():
                dve.wait_ge(S["u_mm"], 1)
                V.tensor_copy(uf, ps[:, 5, 0:NB * 6].rearrange("p (b c) -> p b c", b=NB)).then_inc(S["u_split"], 1)
                V.memset(upos[:, :, 0:1], 0.0).then_inc(S["upos_ready"], 1)
                V.memset(uneg[:, :, 0:1], 1.0).then_inc(S["upos_ready"], 1)
                count = 1
                for k in range(SPLIT):
                    dve.wait_ge(S["u_split"], count)
                    part = upos[:, :, 1 + 6 * k:7 + 6 * k]
                    V.tensor_copy(part, uf).then_inc(S["u_split"], 1)
                    count += 1
                    dve.wait_ge(S["u_split"], count)
                    if k < SPLIT - 1:
                        V.tensor_tensor(uf, uf, part, ALU.subtract).then_inc(S["u_split"], 1)
                        count += 1
                    for s in range(2):
                        V.tensor_copy(uneg[:, :, 1 + 6 * k + 3 * s:4 + 6 * k + 3 * s],
                                      upos[:, :, 4 + 6 * k - 3 * s:7 + 6 * k - 3 * s]).then_inc(S["upos_ready"], 1)

            dve.wait_ge(S["offdiag_in"], 16)

            def pass1(it, first):
                for k in range(RING):
                    jb = RING * it + k
                    dve.wait_ge(loads[k], 16 * (it + 1))
                    d = ring[:, k, bass.ds(jb * P, P)]
                    V.tensor_tensor(d, d, offdiag, ALU.mult).then_inc(S["diag_zeroed"], 1)
                    dve.wait_ge(S["diag_zeroed"], jb + 1)
                    need(dve, S["mask_mm_done"], jb - 1)
                    V.tensor_scalar(pos[:, k % 2, :], ring[:, k, :], 0.0, None, ALU.is_gt).then_inc(S["masks_ready"], 1)
                    V.tensor_scalar(neg[:, k % 2, :], ring[:, k, :], 0.0, None, ALU.is_lt).then_inc(S["masks_ready"], 1)
                    if first and k == 0:
                        split_projections()
            pass1(0, True)
            with dve.Fori(1, NB // RING) as it:
                pass1(it, False)

            def gate_biases():
                dve.wait_ge(S["late_in"], 16 * len(late_loads))
                V.tensor_tensor(gate_b[:, :, :], bih[:, :, 0:2], bhh[:, :, 0:2], ALU.add).then_inc(S["gate_sum"], 1)
                dve.wait_ge(S["gate_sum"], 1)
                V.tensor_scalar(gate_b[:, :, :], gate_b[:, :, :], 0.5, None, ALU.mult).then_inc(S["gate_ready"], 1)

            def prepare(a, tile):
                i, rs = TPC * a + tile, tile_slot(a, tile)
                dve.wait_ge(loads[rs], 16 * tile_loads(a, tile))
                d = ring[:, rs, bass.ds(i * P, P)]
                V.tensor_tensor(d, d, offdiag, ALU.mult).then_inc(S["prep"], 1)
                if not (isinstance(a, int) and a == 0):
                    dve.wait_ge(S["scored"], HEADS * (i - 1))
                elif tile >= ASLOT:
                    dve.wait_ge(S["scored"], last_step(tile - ASLOT) + 1)
                dve.wait_ge(S["prep"], i + 1)
                V.tensor_scalar(mask[:, tile % ASLOT, :], ring[:, rs, :], 0.0, BIG, ALU.is_le,
                                ALU.mult).then_inc(S["mask_ready"], 1)

            dve.wait_ge(S["rows_out"], NC)
            V.tensor_reduce(neg_count[:, :], row_sums[0:1, :], AX_X, ALU.max).then_inc(S["flagged"], 1)
            dve.wait_ge(S["flagged"], 1)
            V.tensor_copy(neg_flag[:, :], neg_count[:, :]).then_inc(S["flagged"], 1)

            def leaky(h):
                for c in range(NC):
                    cols = slice(c * BANK, (c + 1) * BANK)
                    dve.wait_ge(S["scaled"], NC * h + c + 1)
                    V.tensor_tensor(nscore[:, h, cols], ps[:, SPREAD_BANKS[h][c], :], nscore[:, h, cols],
                                    ALU.min).then_inc(S["nscore_ready"], 1)

            def columns():
                dve.wait_ge(S["scaled"], NC * HEADS + 1)
                V.tensor_tensor(scol[:, :, :], cell[:, 0:NB * 2 * HEADS].rearrange("p (b r) -> p b r", b=NB),
                                scol[:, :, :], ALU.min).then_inc(S["bank_read"], 1)

            def score_negative(a, p):
                tile, h = tile_head(a, p)
                rs, e, q = tile_slot(a, tile), p % ASLOT, STEPS * a + p
                done = (5 * NC + 1) * q
                dve.wait_ge(S["plus_scored"], q + 1)
                for c in range(NC):
                    cols = slice(c * BANK, (c + 1) * BANK)
                    need(dve, S["minus_step"], done + 5 * c)
                    V.tensor_scalar(minus[:, :], ring[:, rs, cols], 0.0, BIG, ALU.is_ge,
                                    ALU.mult).then_inc(S["minus_step"], 1)
                    dve.wait_ge(minus_in[c % 2], 16 * (NC // 2 * q + c // 2 + 1))
                    V.scalar_tensor_tensor(out=minus_n[:, c % 2, :], in0=minus_n[:, c % 2, :], scalar=ALPHA,
                                           in1=minus_n[:, c % 2, :], op0=ALU.mult, op1=ALU.min).then_inc(S["minus_step"], 1)
                    dve.wait_ge(S["minus_step"], done + 5 * c + 2)
                    V.tensor_tensor(minus[:, :], minus[:, :], minus_n[:, c % 2, :], ALU.add).then_inc(S["minus_step"], 1)
                    dve.wait_ge(S["minus_step"], done + 5 * c + 3)
                    V.tensor_reduce(nmin4[:, c:c + 1], minus[:, :], AX_X, ALU.min).then_inc(S["minus_step"], 1)
                    dve.wait_ge(S["minus_step"], done + 5 * c + 4)
                    V.tensor_tensor(att[:, e, cols], att[:, e, cols], minus[:, :], ALU.min).then_inc(S["minus_step"], 1)
                dve.wait_ge(S["minus_step"], done + 5 * NC)
                V.tensor_reduce(nmin1[:, :], nmin4[:, :], AX_X, ALU.min).then_inc(S["minus_step"], 1)
                dve.wait_ge(S["minus_step"], done + 5 * NC + 1)
                V.tensor_tensor(nmin[:, h, tile:tile + 1], nmin[:, h, tile:tile + 1], nmin1[:, :], ALU.min).then_inc(S["scored"], 1)

            def score(a, p, signed):
                tile, h = tile_head(a, p)
                rs, ms, e, q, i = tile_slot(a, tile), tile % ASLOT, p % ASLOT, STEPS * a + p, TPC * a + tile
                if h == 0:
                    prepare(a, tile)
                dve.wait_ge(S["mask_ready"], i + 1)
                if p == 0:
                    need(dve, S["nmin_ready"], 0 if isinstance(a, int) and a == 0 else TPC - 1 + a)
                need(dve, S["paused"], q)
                if p >= ASLOT or not (isinstance(a, int) and a == 0):
                    dve.wait_ge(S["exp_done"], q - ASLOT + 1)
                V.memset(pause[:, :], 0.0).then_inc(S["paused"], 1)
                if isinstance(a, int) and a == 0 and tile == 0:
                    for k in range(HEADS) if signed and h == 0 else [h] if not signed else []:
                        leaky(k)
                    dve.wait_ge(S["nscore_ready"], NC * (h + 1))
                V.tensor_tensor_reduce(att[:, e, :], mask[:, ms, :], nscore[:, h, :], 1.0, 3e38, ALU.add, ALU.min,
                                       nmin[:, h, tile:tile + 1]).then_inc(S["plus_scored" if signed else "scored"], 1)
                if signed:
                    score_negative(a, p)

            def set_minima(a, count, tiles=slice(0, TPC)):
                dve.wait_ge(S["scored"], STEPS * a + count)
                if not (isinstance(a, int) and a == 0):
                    dve.wait_ge(S["diag_built"], TPC - 1 + 2 * a - 1)
                V.scalar_tensor_tensor(out=nmin_set[:, :, tiles], in0=nmin[:, :, tiles], scalar=BIG / 2,
                                       in1=nmin[:, :, tiles], op0=ALU.is_lt, op1=ALU.mult).then_inc(S["nmin_ready"], 1)

            def reciprocals(a):
                dve.wait_ge(S["exp_done"], STEPS * a + STEPS)
                if not (isinstance(a, int) and a == 0):
                    dve.wait_ge(S["diag_built"], TPC - 1 + 2 * a)
                V.reciprocal(rden[:, :, :], den[:, :, :]).then_inc(S["rden_ready"], 1)

            def depths(c, j):
                b = NB * c + j
                if j == 0:
                    dve.wait_ge(S["bcast_out"], 2 * HEADS * c + HEADS)
                if j >= ESLOT or not (isinstance(c, int) and c == 0):
                    dve.wait_ge(S["block_done"], b - ESLOT + 1)
                for h in range(vector_heads(j)):
                    last = V.tensor_scalar(weights[:, j % ESLOT, h, :], max_row[:, h, :], scol[:, j, h:h + 1], 0.0,
                                           ALU.add, ALU.max)
                last.then_inc(S["depth"], 1)

            def minus_depths(c, j):
                b = NB * c + j
                if j or not (isinstance(c, int) and c == 0):
                    dve.wait_ge(S["weighted"], b)
                for h in range(HEADS):
                    last = V.tensor_scalar(e_minus[:, h, :], max_row[:, h, :], scol[:, j, HEADS + h:HEADS + h + 1],
                                           0.0, ALU.add, ALU.max)
                last.then_inc(S["minus_depth"], 1)

            def weigh(c, j, signed):
                b = NB * c + j
                slot, e = ASLOT + (j // BPG) % 2, j % ESLOT
                if j % BPG == 0:
                    dve.wait_ge(S["group_ready"], BPG * c + j // BPG + 1)
                adj_block = ring[:, slot, (j % BPG) * BANK:(j % BPG + 1) * BANK]
                dve.wait_ge(S["exp_block"], b + 1)
                if not signed:
                    V.tensor_tensor(weights[:, e, :, :], weights[:, e, :, :],
                                    adj_block.unsqueeze(1).broadcast_to([P, HEADS, BANK]),
                                    ALU.mult).then_inc(S["weighted"], 1)
                    return
                minus_depths(c, j)
                dve.wait_ge(S["minus_block"], b + 1)
                for h in range(HEADS):
                    done = 2 * (HEADS * b + h)
                    plus, other = weights[:, e, h, :], e_minus[:, h, :]
                    V.scalar_tensor_tensor(out=plus, in0=adj_block, scalar=0.0, in1=plus, op0=ALU.max,
                                           op1=ALU.mult).then_inc(S["minus_weight"], 1)
                    V.scalar_tensor_tensor(out=other, in0=adj_block, scalar=0.0, in1=other, op0=ALU.min,
                                           op1=ALU.mult).then_inc(S["minus_weight"], 1)
                    dve.wait_ge(S["minus_weight"], done + 2)
                    last = V.tensor_tensor(plus, plus, other, ALU.add)
                last.then_inc(S["weighted"], 1)

            def divide(c):
                dve.wait_ge(S["bcast_out"], 2 * HEADS * c + 2 * HEADS)
                for h in range(HEADS):
                    dve.wait_ge(S["acc_done"], HEADS * c + h + 1)
                    V.tensor_tensor(rden_row[:, h, :], ps[:, h, :], rden_row[:, h, :], ALU.mult).then_inc(S["acc_read"], 1)

            def gated(c, k):
                base = CELL_OPS * c + (0, 5)[k]
                dve.wait_ge(S["bank_read"], use(c, ("eI", "nI")[k]) + 1)
                V.scalar_tensor_tensor(out=g_r[:, k, :], in0=g_r[:, k, :], scalar=1.0, in1=g_h[:, k, :], op0=ALU.add,
                                       op1=ALU.mult).then_inc(S["cell_vec"], 1)
                dve.wait_ge(S["cell_vec"], base + 1)
                V.scalar_tensor_tensor(out=g_r[:, k, :], in0=g_r[:, k, :], scalar=0.5, in1=g_i[:, k, :], op0=ALU.mult,
                                       op1=ALU.add).then_inc(S["cell_vec"], 1)

            def mixed(c, k):
                base = CELL_OPS * c + (2, 7)[k]
                dve.wait_ge(S["cand_ready"], 2 * c + k + 1)
                V.tensor_tensor(g_i[:, k, :], xT[:, bass.ds(c * BANK, BANK)], g_h[:, k, :],
                                ALU.subtract).then_inc(S["cell_vec"], 1)
                dve.wait_ge(S["bank_read"], use(c, ("eZ", "nZ")[k]) + 1)
                dve.wait_ge(S["cell_vec"], base + 1)
                V.scalar_tensor_tensor(out=g_i[:, k, :], in0=g_z[:, k, :], scalar=1.0, in1=g_i[:, k, :], op0=ALU.add,
                                       op1=ALU.mult).then_inc(S["cell_vec"], 1)
                dve.wait_ge(S["cell_vec"], base + 2)
                if k == 0:
                    V.scalar_tensor_tensor(out=total[:, :], in0=g_i[:, k, :], scalar=0.5, in1=g_h[:, k, :],
                                           op0=ALU.mult, op1=ALU.add).then_inc(S["cell_vec"], 1)
                    return
                V.scalar_tensor_tensor(out=g_i[:, k, :], in0=g_i[:, k, :], scalar=0.5, in1=g_h[:, k, :], op0=ALU.mult,
                                       op1=ALU.add).then_inc(S["cell_vec"], 1)
                dve.wait_ge(S["cell_vec"], base + 3)
                V.tensor_tensor(total[:, :], total[:, :], g_i[:, k, :], ALU.add).then_inc(S["cell_vec"], 1)

            def residual(c):
                tiles = bass.ds(TPC * c, TPC)
                if isinstance(c, int):
                    dve.wait_ge(S["x1_kept"], c)
                dve.wait_ge(S["cell_mm"], use(c, "Ttotal") + 1)
                for b in range(TPC):
                    V.scalar_tensor_tensor(out=x1s[:, b, :], in0=cell[:, b * P:(b + 1) * P],
                                           scalar=diag[:, bass.ds(TPC * c + b, 1)],
                                           in1=row(x_nat[:, bass.ds(TPC * c + b, 1), :]), op0=ALU.mult,
                                           op1=ALU.add).then_inc(S["bank_read" if b == TPC - 1 else "x1_pre"], 1)
                V.scalar_tensor_tensor(out=powers[:, TPC:2 * TPC], in0=diag[:, tiles], scalar=1.0,
                                       in1=rowsum[:, tiles], op0=ALU.add, op1=ALU.add).then_inc(S["x1_moment"], 1)
                dve.wait_ge(S["x1_pre"], 3 * c + 3)
                dve.wait_ge(S["bank_read"], use(c, "Ttotal") + 1)
                for b in range(TPC):
                    V.bn_stats(stats[:, b, :], x1s[:, b, :]).then_inc(S["x1_stat"], 1)
                base = 6 * c
                dve.wait_ge(S["x1_moment"], base + 1)
                V.tensor_scalar(zero_sum[:, :], powers[:, TPC:2 * TPC], 0.0, None, ALU.is_equal).then_inc(S["x1_moment"], 1)
                dve.wait_ge(S["x1_stat"], TPC * c + TPC)
                V.tensor_tensor(mean[:, :], stats[:, :, 1], stats[:, :, 4], ALU.add).then_inc(S["x1_moment"], 1)
                V.tensor_tensor(spread[:, :], stats[:, :, 1], stats[:, :, 4], ALU.subtract).then_inc(S["x1_moment"], 1)
                dve.wait_ge(S["x1_moment"], base + 4)
                V.tensor_tensor(powers[:, TPC:2 * TPC], powers[:, TPC:2 * TPC], zero_sum[:, :],
                                ALU.add).then_inc(S["x1_moment"], 1)
                variance(mean[:, :], spread[:, :], powers[:, 0:TPC], stats[:, :, 2], stats[:, :, 5], "x1_moment",
                         base + 4, "x1_var", 3 * c, "powers_ready")

            def variance(mean_, spread_, var_, m2a, m2b, moment, base, step, at, done):
                V.tensor_scalar(mean_, mean_, 0.5, None, ALU.mult).then_inc(S[moment], 1)
                V.scalar_tensor_tensor(out=spread_, in0=spread_, scalar=0.25, in1=spread_, op0=ALU.mult,
                                       op1=ALU.mult).then_inc(S[step], 1)
                V.tensor_tensor(var_, m2a, m2b, ALU.add).then_inc(S[step], 1)
                dve.wait_ge(S[step], at + 2)
                V.scalar_tensor_tensor(out=var_, in0=var_, scalar=1.0 / P, in1=spread_, op0=ALU.mult,
                                       op1=ALU.add).then_inc(S[step], 1)
                dve.wait_ge(S[step], at + 3)
                dve.wait_ge(S[moment], base + 2 if moment == "x1_moment" else base + 1)
                V.tensor_scalar(var_, var_, EPS, None, ALU.add).then_inc(S[done], 1)

            def normalise(c):
                dve.wait_ge(S["pow_done"], c + 1)
                for b in range(TPC):
                    V.tensor_scalar(x1s[:, b, :], x1s[:, b, :], mean[:, b:b + 1], powers[:, b:b + 1], ALU.subtract,
                                    ALU.mult).then_inc(S["x1_done"], 1)
                V.tensor_scalar(zero_sum[:, :], zero_sum[:, :], -1.0, 1.0, ALU.mult, ALU.add).then_inc(S["r_step"], 1)
                dve.wait_ge(S["r_step"], 3 * c + 1)
                if not (isinstance(c, int) and c == 0):
                    dve.wait_ge(S["bank_read"], use(c, "Ttotal") + 1)
                V.tensor_tensor(r_chunk[:, :], powers[:, TPC:2 * TPC], zero_sum[:, :], ALU.mult).then_inc(S["r_step"], 1)
                dve.wait_ge(S["r_step"], 3 * c + 2)
                V.tensor_copy(r_all[:, bass.ds(TPC * c, TPC)], r_chunk[:, :]).then_inc(S["r_step"], 1)

            def body(c, signed, first, last_chunk):
                if first:
                    dve.wait_ge(S["minus_stored"], 16)
                    dve.wait_ge(S["bank_read"], 1)
                depths(c, 0)
                depths(c, 1)
                for j in range(NB):
                    if j < STEPS and not last_chunk:
                        score(c + 1, j, signed)
                    if j == STEPS - 1 and not last_chunk:
                        set_minima(c + 1, STEPS)
                    weigh(c, j, signed)
                    if j == 0 and not first:
                        divide(c - 1)
                    if j + 2 < NB:
                        depths(c, j + 2)
                    if j == STEPS + 1 and not last_chunk:
                        reciprocals(c + 1)
                    if first:
                        continue
                    if j == 5:
                        gated(c - 1, 0)
                    if j == 7:
                        mixed(c - 1, 0)
                    if j == 9:
                        gated(c - 1, 1)
                    if j == 10:
                        mixed(c - 1, 1)
                    if j == 11:
                        residual(c - 1)
                    if j == 12:
                        normalise(c - 1)

            def middle(signed):
                for p in range(STEPS):
                    score(0, p, signed)
                    if p == 9:
                        columns()
                        gate_biases()
                    tile = tile_head(0, p)[0]
                    if p == last_step(tile):
                        set_minima(0, p + 1, slice(tile, tile + 1))
                reciprocals(0)
                body(0, signed, True, False)
                with dve.Fori(1, NC - 1) as it:
                    body(it, signed, False, False)
                body(NC - 1, signed, False, True)
            with dve.If(negatives(dve) > 0):
                middle(True)
            with dve.Else():
                middle(False)
            divide(NC - 1)
            for k in range(2):
                gated(NC - 1, k)
                mixed(NC - 1, k)
            residual(NC - 1)
            normalise(NC - 1)

            def shift_chunk(c):
                tiles = slice(TPC * c, TPC * (c + 1))
                dve.wait_ge(S["pow2_done"], c + 1)
                V.scalar_tensor_tensor(out=shift[:, tiles], in0=mean2[:, tiles], scalar=-1.0, in1=rstd2[:, tiles],
                                       op0=ALU.mult, op1=ALU.mult).then_inc(S["fin_shift"], 1)

            dve.wait_ge(S["x1_kept"], NC)
            for c in range(NC):
                tiles = slice(TPC * c, TPC * (c + 1))
                xc = x2[:, tiles, :].rearrange("p b f -> p (b f)")
                dve.wait_ge(S["out_tr"], c + 1)
                V.tensor_tensor(xc, ps[:, 4 + c, :], gmat[:, tiles, :].rearrange("p b f -> p (b f)"),
                                ALU.add).then_inc(S["fin_sum"], 1)
                dve.wait_ge(S["fin_sum"], c + 1)
                for i in range(TPC * c, TPC * (c + 1)):
                    V.scalar_tensor_tensor(out=x2[:, i, :], in0=x2[:, i, :], scalar=r_all[:, i:i + 1], in1=x1[:, i, :],
                                           op0=ALU.mult, op1=ALU.add).then_inc(S["x2_pre"], 1)
                for i in range(TPC * c, TPC * (c + 1)):
                    dve.wait_ge(S["x2_pre"], i + 1)
                    V.bn_stats(stats2[:, i, :], x2[:, i, :]).then_inc(S["fin_stat"], 1)
                dve.wait_ge(S["fin_stat"], TPC * (c + 1))
                V.tensor_tensor(mean2[:, tiles], stats2[:, tiles, 1], stats2[:, tiles, 4], ALU.add).then_inc(S["fin_moment"], 1)
                V.tensor_tensor(spread2[:, tiles], stats2[:, tiles, 1], stats2[:, tiles, 4],
                                ALU.subtract).then_inc(S["fin_moment"], 1)
                dve.wait_ge(S["fin_moment"], 3 * c + 2)
                variance(mean2[:, tiles], spread2[:, tiles], var2[:, tiles], stats2[:, tiles, 2], stats2[:, tiles, 5],
                         "fin_moment", 3 * c + 2, "fin_step", 3 * c, "fin_var")
                if c:
                    shift_chunk(c - 1)
            shift_chunk(NC - 1)

        @block.tensor
        def _(pe):
            mm = nc.tensor.matmul

            def projections():
                pe.wait_ge(S["prep_in"], 16 * len(prep_loads))
                for h in range(HEADS):
                    last = mm(ps[:, 4, 2 * h:2 * h + 2], gatWT[:, h, :], gata[:, h, :], start=True, stop=True)
                last.then_inc(S["wa_mm"], 1)
                pe.wait_ge(S["wa_ready"], 1)
                wa_cols = wa[:, :, :].rearrange("p s h -> p (s h)")
                for b in range(NB):
                    last = mm(ps[:, 5, 6 * b:6 * b + 6], xT[:, b * P:(b + 1) * P], wa_cols, start=True, stop=True)
                last.then_inc(S["u_mm"], 1)

            def pass1(it, first):
                for k in range(RING):
                    jb = RING * it + k
                    start = first and k == 0
                    if start:
                        projections()
                    pe.wait_ge(S["x_staged"], jb + 1)
                    pe.wait_ge(S["diag_zeroed"], jb + 1)
                    mm(ns_bank, x_st[:, k, :], ring[:, k, EARLY * BANK:N], start=start, stop=True,
                       skip_group_check=True)
                    if start:
                        pe.wait_ge(S["upos_ready"], 2 * SPLIT + 2)
                    for sgn, (u, m) in enumerate(((upos, pos), (uneg, neg))):
                        pe.wait_ge(S["masks_ready"], 2 * jb + 1 + sgn)
                        for c in range(NC):
                            last = mm(ps[0:ROWS, 4 + c, :], row(u[:, bass.ds(jb, 1), 0:ROWS]),
                                      m[:, k % 2, c * BANK:(c + 1) * BANK], start=start and sgn == 0, stop=True,
                                      skip_group_check=True)
                    last.then_inc(S["mask_mm_done"], 1)
            pass1(0, True)
            with pe.Fori(1, NB // RING) as it:
                pass1(it, False)
            pe.wait_ge(S["consts_in"], 16 * len(const_loads))

            def spread_scores(h):
                for c in range(NC):
                    if h == 0:
                        pe.wait_ge(S["rows_out"], c + 1)
                    elif h == 2:
                        pe.wait_ge(S["nscore_ready"], c + 1)
                    elif SPREAD_BANKS[h][c] == 3:
                        pe.wait_ge(S["ns_early"], 1)
                    mm(ps[:, SPREAD_BANKS[h][c], :], spread_sel[:, h, :], score_rows[:, c * BANK:(c + 1) * BANK],
                       start=True, stop=True).then_inc(S["spread_mm"], 1)
            spread_scores(0)
            spread_scores(1)
            spread_scores(2)
            for c in range(NC):
                pe.wait_ge(S["nscore_ready"], NC + c + 1)
                mm(ps[0:HEADS, MINUS_BANKS[c], :], sum_sel[:, HEADS:2 * HEADS], score_rows[:, c * BANK:(c + 1) * BANK],
                   start=True, stop=True).then_inc(S["minus_mm"], 1)
            pe.wait_ge(S["minus_out"], 3)
            for b in range(NB):
                last = mm(cell[:, b * 2 * HEADS:(b + 1) * 2 * HEADS], score_rows[:, b * P:(b + 1) * P], sum_sel,
                          start=True, stop=True)
            last.then_inc(S["cell_mm"], 1)

            def spread(c, k):
                n = 2 * HEADS * c + k
                pe.wait_ge(S["diag_built"], TPC + 2 * c + k // HEADS)
                if k >= HEADS:
                    before = max(m for m in range(k) if BODY_BANKS[m] == BODY_BANKS[k])
                    pe.wait_ge(S["bcast_out"], 2 * HEADS * c + before + 1)
                else:
                    need(pe, S["bcast_out"], 2 * HEADS * c)
                    if BODY_BANKS[k] == 6:
                        need(pe, S["s_evac"], c - 1)
                mm(ps[:, BODY_BANKS[k], :], ones, spread_src[:, k % HEADS, :, :].rearrange("p t k -> p (t k)"),
                   start=True, stop=True).then_inc(S["bcast_mm"], 1)

            def product(c, j, sums, first):
                slot, e = ASLOT + (j // BPG) % 2, j % ESLOT
                pe.wait_ge(S["weighted"], NB * c + j + 1)
                for h in range(HEADS):
                    if j == 0 and not first:
                        pe.wait_ge(S["acc_read"], HEADS * (c - 1) + h + 1)
                    last = mm(ps[:, h, :], x_nat[:, j, :], weights[:, e, h, :], start=j == 0, stop=j == NB - 1,
                              skip_group_check=True)
                    if j == NB - 1:
                        last.then_inc(S["acc_done"], 1)
                if not sums:
                    if j < NB - 1:
                        last.then_inc(S["block_done"], 1)
                    return
                if j == 0 and not first:
                    pe.wait_ge(S["ns_ready"], c)
                mm(ns_bank, x_nat[:, j, :], ring[:, slot, (j % BPG) * BANK:(j % BPG + 1) * BANK], start=j == 0,
                   stop=j == NB - 1, skip_group_check=True).then_inc(S["block_done"], 1)

            def project(c):
                pe.wait_ge(S["bcast_out"], 2 * HEADS * min(c + 1, NC - 1) + HEADS if isinstance(c, int)
                           else 2 * HEADS * c + 3 * HEADS)
                for h in range(HEADS):
                    pe.wait_ge(S["acc_read"], HEADS * c + h + 1)
                    mm(s_ps, gatW[:, h, :], rden_row[:, h, :], start=h == 0, stop=h == HEADS - 1,
                       skip_group_check=True).then_inc(S["s_mm"], 1)

            def cell_use(c, name):
                need(pe, S["bank_read"], use(c, name))
                if name[0] != "T":
                    k, g = "en".index(name[0]), name[1]
                    cols = bass.ds(c * BANK, BANK)
                    gate = slice(GATE_COLS[g] * P, (GATE_COLS[g] + 1) * P)
                    if name == "eR" and not (isinstance(c, int) and c == EARLY):
                        pe.wait_ge(S["ns_ready"], c + 1)
                    if name == "nR":
                        pe.wait_ge(S["s_evac"], c + 1)
                    inp = (nsT, supT)[k]
                    if g != "H":
                        last = mm(cell, wih[:, k, gate], inp[:, cols], start=True, stop=g == "I")
                    if g != "I":
                        last = mm(cell, whh[:, k, gate], xT[:, cols], start=g == "H", stop=True)
                elif name == "Ttotal":
                    pe.wait_ge(S["cell_vec"], CELL_OPS * (c + 1))
                    for b in range(TPC):
                        last = nc.tensor.transpose(cell[:, b * P:(b + 1) * P], total[:, b * P:(b + 1) * P], ident[:, :])
                elif name == "Tx1":
                    pe.wait_ge(S["x1_done"], TPC * c + TPC)
                    for b in range(TPC):
                        last = nc.tensor.transpose(cell[:, b * P:(b + 1) * P], x1s[:, b, :], ident[:, :])
                else:
                    for b in range(TPC):
                        mm(cell[:, b * P:(b + 1) * P], x1T[:, b * P:(b + 1) * P], l1WT[:, :], start=True, stop=False,
                           skip_group_check=True)
                        last = mm(cell[:, b * P:(b + 1) * P], ones_row[:, :], l1b[:, :], start=False, stop=True,
                                  skip_group_check=True)
                last.then_inc(S["cell_mm"], 1)

            def body(c, first, last_chunk):
                for j in range(NB):
                    product(c, j, not last_chunk, first)
                    if j == 0 and not first:
                        project(c - 1)
                    if 8 <= j < 8 + HEADS:
                        spread(c, j - 8 + HEADS)
                    if not first:
                        for name in ORDER:
                            if PE_AT[name] == j:
                                cell_use(c - 1, name)
                    if j == 11 and not last_chunk:
                        spread(c + 1, 0)
                        spread(c + 1, 1)
                        spread(c + 1, 2)
            pe.wait_ge(S["nscore_ready"], HEADS * NC)
            pe.wait_ge(S["late_in"], 16 * len(late_loads))
            for tile in range(TPC):
                pe.wait_ge(S["diag_built"], tile + 1)
                for h in range(HEADS):
                    last = mm(ps[:, BODY_BANKS[h], tile * P:(tile + 1) * P], ones, spread_src[:, h, tile, :],
                              start=True, stop=True)
                    if tile == TPC - 1:
                        last.then_inc(S["bcast_mm"], 1)
            body(0, True, False)
            with pe.Fori(1, NC - 1) as it:
                body(it, False, False)
            body(NC - 1, False, True)

            beside = {0: "eR", 1: "eH", 2: "eI", 3: "eZ", 4: "nR", 5: "nH", 6: "nI", 7: "nZ", 12: "Ttotal", 16: "Tx1",
                      18: "Tproj"}
            pe.wait_ge(S["acc_read"], HEADS * NC)
            pe.wait_ge(S["ns_ready"], NC - 1)
            for jb in range(NB - LAST):
                if jb % TPC == 0:
                    pe.wait_ge(S["bank_read"], use(jb // TPC, "Tproj") + 1)
                pe.wait_ge(loads[jb % RING], 16 * (before_conv(jb % RING) + jb // RING + 1))
                for c in range(NC):
                    last = mm(ps[:, c, :], gmat[:, jb, :], ring[:, jb % RING, c * BANK:(c + 1) * BANK],
                              start=jb == 0, stop=False, skip_group_check=True)
                    if c == NC - 1:
                        last.then_inc(S["conv_done"], 1)
                    if jb == 0 and c == 1:
                        project(NC - 1)
                    if c % 2 and 2 * jb + c // 2 in beside:
                        cell_use(NC - 1, beside[2 * jb + c // 2])
            for k in range(RING - LAST, RING):
                pe.wait_ge(loads[k], 16 * (before_conv(k) + NB // RING))
            for c in range(NC + 1):
                if c < NC:
                    for jb in range(NB - LAST, NB):
                        last = mm(ps[:, c, :], gmat[:, jb, :], ring[:, jb % RING, c * BANK:(c + 1) * BANK],
                                  start=False, stop=jb == NB - 1, skip_group_check=True)
                    last.then_inc(S["conv_out"], 1)
                if c:
                    pe.wait_ge(S["outT_done"], c)
                    for b in range(TPC):
                        last = nc.tensor.transpose(ps[:, 3 + c, b * P:(b + 1) * P],
                                                   outT[:, (c - 1) * BANK + b * P:(c - 1) * BANK + (b + 1) * P],
                                                   ident[:, :])
                    last.then_inc(S["out_tr"], 1)


def kernel(x, adj, L0_gnn_gat_W, L0_gnn_gat_a, L0_gnn_edge_Wih, L0_gnn_edge_Whh, L0_gnn_edge_bih, L0_gnn_edge_bhh,
           L0_gnn_node_Wih, L0_gnn_node_Whh, L0_gnn_node_bih, L0_gnn_node_bhh, L1_gnn_W, L1_gnn_b):
    import concourse.bacc as bacc
    from concourse.bass_utils import run_bass_kernel_spmd

    C = np.ascontiguousarray
    adj = np.asarray(adj)
    x = np.asarray(x)
    eye = np.eye(P, dtype=np.float32)
    sum_sel = np.zeros((ROWS, 2 * HEADS), np.float32)
    spread_sel = np.zeros((ROWS, HEADS, P), np.float32)
    for r in range(1, ROWS):
        sum_sel[r, (r - 1) % (2 * HEADS)] = -1.0
        if (r - 1) % (2 * HEADS) < HEADS:
            spread_sel[r, (r - 1) % (2 * HEADS), :] = -1.0
    diag_masks = np.ones((P, 2 * NC - 1, P), np.float32)
    diag_masks[:, NC - 1, :] -= eye
    arrays = {
        "x": C(x), "xT": C(x.T), "adj": C(adj), "adjT": C(adj.T),
        "adj_diag": C(adj.diagonal().reshape(NB, P).T),
        "gat_W": C(L0_gnn_gat_W), "gat_WT": C(np.asarray(L0_gnn_gat_W).transpose(0, 2, 1)),
        "gat_aT": C(np.asarray(L0_gnn_gat_a).reshape(HEADS, 2, P).transpose(2, 0, 1)),
        "edge_WihT": C(np.asarray(L0_gnn_edge_Wih).T), "edge_WhhT": C(np.asarray(L0_gnn_edge_Whh).T),
        "node_WihT": C(np.asarray(L0_gnn_node_Wih).T), "node_WhhT": C(np.asarray(L0_gnn_node_Whh).T),
        "edge_bih": C(np.asarray(L0_gnn_edge_bih).reshape(3, P).T),
        "edge_bhh": C(np.asarray(L0_gnn_edge_bhh).reshape(3, P).T),
        "node_bih": C(np.asarray(L0_gnn_node_bih).reshape(3, P).T),
        "node_bhh": C(np.asarray(L0_gnn_node_bhh).reshape(3, P).T),
        "l1WT": C(np.asarray(L1_gnn_W).T), "l1b": C(np.asarray(L1_gnn_b).reshape(1, P)),
        "ident": eye, "diag_masks": diag_masks, "sum_sel": sum_sel, "spread_sel": spread_sel,
        "ones_row": np.ones((1, P), np.float32),
    }
    nc = bacc.Bacc("TRN2", target_bir_lowering=False, num_devices=1)
    t = {k: nc.dram_tensor(f"in_{k}", a.shape, F32, kind="ExternalInput").ap() for k, a in arrays.items()}
    t["minus_rows"] = nc.dram_tensor("minus_rows", (HEADS, N), F32, kind="Internal").ap()
    t["out"] = nc.dram_tensor("out", (N, P), F32, kind="ExternalOutput").ap()
    build(nc, t)
    r = run_bass_kernel_spmd(nc, [{f"in_{k}": a for k, a in arrays.items()}], core_ids=[0])
    return r.results[0]["out"]
```
